# Optimizing a Trainium2 kernel written in Bass

```python
import numpy as np
import jax
import jax.numpy as jnp

def _softmax(x, axis=-1):
    return jax.nn.softmax(x, axis=axis)

def _gelu(x):
    return jax.nn.gelu(x, approximate=True)

def _silu(x):
    return jax.nn.silu(x)

def _sigmoid(x):
    return jax.nn.sigmoid(x)

def _layernorm(x, axis=-1, eps=1e-05):
    m = jnp.mean(x, axis=axis, keepdims=True)
    v = jnp.var(x, axis=axis, keepdims=True)
    return (x - m) / jnp.sqrt(v + eps)

def _scatter_add(tgt, idx, src, axis=0):
    return tgt.at[idx].add(src)

def _segment_sum(src, seg, n):
    return jax.ops.segment_sum(src, seg, n)
kernel_name = 'mk_flamingo_gated_d1_seqx_r8_868bf6'

def setup_inputs(seed: int=0):
    np.random.seed(seed)
    _w = jnp.asarray

    def _rec_inputs():
        import jax
        import jax.numpy as jnp
        _rk = jax.random.key(seed)
        x = -7.109e-05 + 0.9999 * jax.random.normal(jax.random.fold_in(_rk, 1), (4, 256, 256), jnp.float32)
        _lenS = 256 - jax.random.randint(jax.random.fold_in(_rk, 7), (4,), 0, max(1, 256 // 4) + 1, jnp.int32)
        _lenS2 = 256 - jax.random.randint(jax.random.fold_in(_rk, 8), (4,), 0, max(1, 256 // 4) + 1, jnp.int32)
        _ctx_512P = jax.random.normal(jax.random.fold_in(_rk, 11), (4, 16, 64), jnp.float32)
        _ctx_512c = jax.random.dirichlet(jax.random.fold_in(_rk, 511), 0.3 * jnp.ones((16,), jnp.float32), (4, 256))
        _ctx_512t = jnp.einsum('bsk,bkd->bsd', _ctx_512c, _ctx_512P)
        _ctx_512t = _ctx_512t * jax.lax.rsqrt(jnp.mean(jnp.square(_ctx_512t)) + 1e-12) * 0.953939
        ctx_512 = 2.81802e-05 + 1.00001 * (_ctx_512t + 0.3 * jax.random.normal(jax.random.fold_in(_rk, 611), (4, 256, 64), jnp.float32))
        _g = jax.random.normal(jax.random.fold_in(_rk, 9001), (2, 1), jnp.float32)
        _g = jnp.sign(_g) * jnp.maximum(jnp.abs(_g), 1.0) + (_g == 0) * 1.0
        g_xattn = _g[0]
        g_ffn = _g[1]
        return (x, ctx_512, g_xattn, g_ffn)
    x, ctx_512, g_xattn, g_ffn = _rec_inputs()

    def _L0_xattn_setup():
        import jax, jax.numpy as jnp
        import numpy as np
        EPS = 1e-06
        IMAGE_DIMS = 256
        key = jax.random.key(seed)
        k1, k2, k3 = jax.random.split(key, 3)
        B, I, J, D = (16, 256, 256, 64)
        p = jax.random.normal(k1, (B, I, J), dtype=jnp.float32)
        k_v = jax.random.normal(k2, (B, J, D), dtype=jnp.float32)
        W_k = jax.random.normal(k3, (D, D), dtype=jnp.float32) * (1.0 / np.sqrt(D))
        b_k = jnp.zeros((D,), dtype=jnp.float32)
        ln_gamma = jnp.ones((J,), dtype=jnp.float32)
        ln_beta = jnp.zeros((J,), dtype=jnp.float32)
        return {'p': p, 'k_v': k_v, 'W_k': W_k, 'b_k': b_k, 'ln_gamma': ln_gamma, 'ln_beta': ln_beta}
    _L0_xattn_all = _L0_xattn_setup()
    _L0_xattn_in = {k: v for k, v in _L0_xattn_all.items() if k in ('W_k', 'b_k', 'ln_gamma', 'ln_beta')}
    del _L0_xattn_all

    def _L0_ffn_setup():
        import jax, jax.numpy as jnp
        import numpy as np
        B, S, H = (4, 256, 256)
        INTER = 512
        E = 8
        TOPK = 2
        SHARED_I = INTER * 2

        def moe_forward(hidden_states, router_w, w1, w2, w_gate, w_up, w_down):
            b, s, h = hidden_states.shape
            x = hidden_states.reshape(-1, h)
            T = x.shape[0]
            logits = x @ router_w
            top_logits, top_indices = jax.lax.top_k(logits, TOPK)
            scores = jax.nn.softmax(top_logits, axis=-1)
            flat_idx = top_indices.reshape(-1)
            sorted_pos = jnp.argsort(flat_idx, stable=True)
            permuted = x[sorted_pos // TOPK]
            expert_ids = flat_idx[sorted_pos]
            out = jnp.zeros((T * TOPK, h), x.dtype)
            for e in range(E):
                mask = (expert_ids == e)[:, None]
                f1 = permuted * mask @ w1[e]
                g, u = jnp.split(f1, 2, axis=-1)
                act = jax.nn.silu(g) * u
                out = out + jnp.where(mask, act @ w2[e], 0.0)
            unperm = jnp.zeros_like(out).at[sorted_pos].set(out)
            combined = (unperm.reshape(T, TOPK, h) * scores[..., None]).sum(axis=1)
            shared = jax.nn.silu(x @ w_gate) * (x @ w_up) @ w_down
            return (combined + shared).reshape(b, s, h)
        key = jax.random.key(seed)
        ks = jax.random.split(key, 7)
        s = 0.02
        return {'hidden_states': jax.random.normal(ks[0], (B, S, H), jnp.float32), 'router_w': jax.random.normal(ks[1], (H, E), jnp.float32) * s, 'w1': jax.random.normal(ks[2], (E, H, 2 * INTER), jnp.float32) * s, 'w2': jax.random.normal(ks[3], (E, INTER, H), jnp.float32) * s, 'w_gate': jax.random.normal(ks[4], (H, SHARED_I), jnp.float32) * s, 'w_up': jax.random.normal(ks[5], (H, SHARED_I), jnp.float32) * s, 'w_down': jax.random.normal(ks[6], (SHARED_I, H), jnp.float32) * s}
    _L0_ffn_all = _L0_ffn_setup()
    _L0_ffn_in = {k: v for k, v in _L0_ffn_all.items() if k in ('router_w', 'w1', 'w2', 'w_gate', 'w_up', 'w_down')}
    del _L0_ffn_all
    return {'x': x, 'ctx_512': ctx_512, 'g_xattn': g_xattn, 'g_ffn': g_ffn, 'L0_xattn_W_k': _L0_xattn_in['W_k'], 'L0_xattn_b_k': _L0_xattn_in['b_k'], 'L0_xattn_ln_gamma': _L0_xattn_in['ln_gamma'], 'L0_xattn_ln_beta': _L0_xattn_in['ln_beta'], 'L0_ffn_router_w': _L0_ffn_in['router_w'], 'L0_ffn_w1': _L0_ffn_in['w1'], 'L0_ffn_w2': _L0_ffn_in['w2'], 'L0_ffn_w_gate': _L0_ffn_in['w_gate'], 'L0_ffn_w_up': _L0_ffn_in['w_up'], 'L0_ffn_w_down': _L0_ffn_in['w_down']}

def reference(x, ctx_512, g_xattn, g_ffn, L0_xattn_W_k, L0_xattn_b_k, L0_xattn_ln_gamma, L0_xattn_ln_beta, L0_ffn_router_w, L0_ffn_w1, L0_ffn_w2, L0_ffn_w_gate, L0_ffn_w_up, L0_ffn_w_down):
    import jax
    import jax.numpy as jnp

    def _L0_xattn_ref(p, k_v, W_k, b_k, ln_gamma, ln_beta):
        import jax, jax.numpy as jnp
        import numpy as np
        EPS = 1e-06
        IMAGE_DIMS = 256
        kv = k_v @ W_k.T + b_k
        out = jnp.einsum('bij,bjd->bid', p, kv)
        scale = IMAGE_DIMS ** (-0.5)
        sim = jnp.einsum('bid,bjd->bij', out, kv) * scale
        mu = jnp.mean(sim, axis=-1, keepdims=True)
        var = jnp.var(sim, axis=-1, keepdims=True)
        sim = (sim - mu) * jax.lax.rsqrt(var + EPS) * ln_gamma + ln_beta
        attn = jax.nn.softmax(sim, axis=-1)
        return attn

    def _L0_ffn_ref(hidden_states, router_w, w1, w2, w_gate, w_up, w_down):
        import jax, jax.numpy as jnp
        import numpy as np
        B, S, H = (4, 256, 256)
        INTER = 512
        E = 8
        TOPK = 2
        SHARED_I = INTER * 2

        def moe_forward(hidden_states, router_w, w1, w2, w_gate, w_up, w_down):
            b, s, h = hidden_states.shape
            x = hidden_states.reshape(-1, h)
            T = x.shape[0]
            logits = x @ router_w
            top_logits, top_indices = jax.lax.top_k(logits, TOPK)
            scores = jax.nn.softmax(top_logits, axis=-1)
            flat_idx = top_indices.reshape(-1)
            sorted_pos = jnp.argsort(flat_idx, stable=True)
            permuted = x[sorted_pos // TOPK]
            expert_ids = flat_idx[sorted_pos]
            out = jnp.zeros((T * TOPK, h), x.dtype)
            for e in range(E):
                mask = (expert_ids == e)[:, None]
                f1 = permuted * mask @ w1[e]
                g, u = jnp.split(f1, 2, axis=-1)
                act = jax.nn.silu(g) * u
                out = out + jnp.where(mask, act @ w2[e], 0.0)
            unperm = jnp.zeros_like(out).at[sorted_pos].set(out)
            combined = (unperm.reshape(T, TOPK, h) * scores[..., None]).sum(axis=1)
            shared = jax.nn.silu(x @ w_gate) * (x @ w_up) @ w_down
            return (combined + shared).reshape(b, s, h)
        return moe_forward(hidden_states, router_w, w1, w2, w_gate, w_up, w_down)
    x = x + jnp.tanh(g_xattn[0]) * _L0_xattn_ref(_layernorm(x, axis=-1), ctx_512, L0_xattn_W_k, L0_xattn_b_k, L0_xattn_ln_gamma, L0_xattn_ln_beta)
    x = x + jnp.tanh(g_ffn[0]) * _L0_ffn_ref(_layernorm(x, axis=-1), L0_ffn_router_w, L0_ffn_w1, L0_ffn_w2, L0_ffn_w_gate, L0_ffn_w_up, L0_ffn_w_down)
    return x

_drawn_inputs = setup_inputs


def setup_inputs(seed=0):
    import zlib

    import numpy as np

    out = dict(_drawn_inputs(seed))
    spreads = {'L0_xattn_b_k': (0.0, 0.8),
     'L0_xattn_ln_gamma': (1.0, 0.6),
     'L0_xattn_ln_beta': (0.0, 0.8)}
    factors = {'ctx_512': 8.0,
     'L0_xattn_W_k': 8.0,
     'L0_ffn_router_w': 4.052,
     'L0_ffn_w1': 3.52,
     'L0_ffn_w2': 3.524}
    for name, (base, spread) in spreads.items():
        noise = np.random.default_rng([zlib.crc32(name.encode()), seed]).standard_normal(out[name].shape)
        drawn = base * np.exp(spread * noise) if base else spread * noise
        out[name] = jnp.asarray(drawn.astype(out[name].dtype))
    for name, factor in factors.items():
        out[name] = (out[name] * factor).astype(out[name].dtype)
    return out
```

```python
import concourse.bass as bass
from concourse import mybir
from contextlib import ExitStack


def gated_attention_moe(nc, x, xT, ctxT, wkT, bk, gamma, beta, g_att, g_ffn, rw, w1, w2, wg, wu, wd, out):
    f32 = mybir.dt.float32
    i32 = mybir.dt.int32
    u32 = mybir.dt.uint32
    ALU = mybir.AluOpType
    ACT = mybir.ActivationFunctionType
    AX = mybir.AxisListType

    P = 128
    T, D = x.shape
    NT = T // P
    HT = NT // 2
    KC = D // P
    C = ctxT.shape[0]
    NBATCH = 4
    TB = T // NBATCH
    E = rw.shape[1]
    TOPK = 2
    F2 = w1.shape[2]
    F = F2 // 2
    FC = F // P
    SI = wg.shape[1]
    SC = SI // P
    NB = (TOPK * T + E * (P - 1)) // P
    SCALE = float(D) ** -0.5
    LN_EPS, SIM_EPS = 1e-5, 1e-6
    MAGIC = float(0x5F3759DF)

    x_t = x.rearrange("(t p) d -> p t d", p=P)
    out_t = out[0:T, :].rearrange("(t p) d -> p t d", p=P)
    h_dram = nc.dram_tensor("h_rows", (T + P, D), f32).ap()
    h_t = h_dram[0:T, :].rearrange("(t p) d -> p t d", p=P)

    ctx = ExitStack()
    with ctx:
        def sb(name, shape, dt=f32):
            return ctx.enter_context(nc.sbuf_tensor(name, shape, dt))

        def sem(name):
            return ctx.enter_context(nc.semaphore(name))

        bank = [ctx.enter_context(nc.psum_tensor(f"bank{i}", [P, 512], f32)) for i in range(8)]

        x_sb = sb("x_sb", [P, NT, D])
        xT_sb = sb("xT_sb", [P, KC, T])
        h_sb = xT_sb[:, :, :].rearrange("p k (a d) -> p (k a) d", d=D)
        early = sb("early", [P, 4, T])
        ctx_sb, ctxc_sb, kvT_sb, oT_sb = early[0:C + 1, 0, :], early[0:C, 1, :], early[0:C, 2, :], early[0:C, 3, :]
        saT = early[:, :, :].rearrange("p a (b n) -> p (a b) n", n=512)
        wk_sb = sb("wk_sb", [C + 1, C])
        gam_sb = sb("gam_sb", [P, D])
        bet_sb = sb("bet_sb", [P, D])
        gates = sb("gates", [P, 2])
        tanhs = sb("tanhs", [P, 2])
        rw_sb = sb("rw_sb", [P, KC, E])
        w1_sb = sb("w1_sb", [P, E, KC, F2])
        w2_sb = sb("w2_sb", [P, E, FC, D])
        wg_sb = sb("wg_sb", [P, KC, SI])
        wu_sb = sb("wu_sb", [P, KC, SI])
        wd_sb = sb("wd_sb", [P, SC, D])
        ident = sb("ident", [P, P])
        before = sb("before", [P, P])
        ones = sb("ones", [P, P])
        zeros = sb("zeros", [P, D])
        iota_e = sb("iota_e", [P, E])
        iota_b = sb("iota_b", [P, NB])
        iota_j = sb("iota_j", [P, P])
        row_of = sb("row_of", [P, 1])
        back_of = sb("back_of", [P, NT])
        steps = sb("steps", [P, E, NT])
        upto = sb("upto", [P, E, E])
        cmean = sb("cmean", [C, NBATCH])
        kvc_sb = sb("kvc_sb", [P, NT, C])
        stats = sb("stats", [P, NT, 6])
        mvx = sb("mvx", [P, NT, 2])
        mvs = sb("mvs", [P, NT, 2])
        mvh = sb("mvh", [P, NT, 2])
        var = sb("var", [P, NT])
        r_y = sb("r_y", [P, NT])
        r_p = sb("r_p", [P, NT])
        r_q = sb("r_q", [P, NT])
        rx = sb("rx", [P, NT])
        rs = sb("rs", [P, NT])
        rh = sb("rh", [P, NT])
        z_sb = sb("z_sb", [P, HT, D])
        nmax = sb("nmax", [P, NT])
        esum = sb("esum", [P, NT])
        einv = sb("einv", [P, NT])
        hT_sb = sb("hT_sb", [P, KC, T])
        logit = sb("logit", [P, NT, E])
        top = sb("top", [P, NT, 8])
        topi = sb("topi", [P, NT, 8], u32)
        idxf = sb("idxf", [P, TOPK, NT])
        hot_e = sb("hot_e", [P, TOPK, NT, E])
        picks = sb("picks", [P, NT + 1, E])
        dlt = sb("dlt", [P, NT])
        edlt = sb("edlt", [P, NT])
        score = sb("score", [P, TOPK, NT])
        pre = sb("pre", [P, NT + 1, E])
        over = sb("over", [P, E, NT])
        nblk = sb("nblk", [P, E])
        cum = sb("cum", [P, E, E])
        bend = sb("bend", [P, E])
        sstart = sb("sstart", [P, E])
        slotp = sb("slotp", [P, TOPK, NT, E])
        slotf = sb("slotf", [P, TOPK * NT])
        sloti = sb("sloti", [P, TOPK * NT], i32)
        posi = sb("posi", [P, 2, TOPK * NT], i32)
        posf = sb("posf", [P, 2, TOPK * NT])
        hot_b = sb("hot_b", [P, TOPK * NT, NB])
        load = sb("load", [P, TOPK * NT, 2, NB])
        hot_j = sb("hot_j", [P, TOPK * NT, P])
        tab = sb("tab", [P, 2, NB])
        padrow = sb("padrow", [P, NB])
        rows = sb("rows", [P, NB], i32)
        bge = sb("bge", [P, NB, E])
        bexp = sb("bexp", [P, NB])
        bexpi = sb("bexpi", [P, NB], i32)
        sg = sb("sg", [P, 512])
        xg = [sb(f"xg{i}", [P, D]) for i in range(3)]
        xgT = [sb(f"xgT{i}", [P, D]) for i in range(3)]
        act = sb("act", [P, F])
        actT = sb("actT", [P, F])
        ysb = [sb(f"ysb{i}", [P, D]) for i in range(3)]

        small_in, x_in, xT_in, sw_in, w1_in, w2_in = (sem(n) for n in ("small_in", "x_in", "xT_in", "sw_in", "w1_in", "w2_in"))
        consts, pool_step, ones_row = sem("consts"), sem("pool_step"), sem("ones_row")
        dve_step, act_step = sem("dve_step"), sem("act_step")
        ctxc_ready, kvT_done, kvc_done, kvT_ready, kvc_ready = (sem(n) for n in ("ctxc_ready", "kvT_done", "kvc_done", "kvT_ready", "kvc_ready"))
        oT_done, oT_ready, sim_done, sim_read = (sem(n) for n in ("oT_done", "oT_ready", "sim_done", "sim_read"))
        tanh_ready, max_ready, exp_ready, h_ready, h_out = (sem(n) for n in ("tanh_ready", "max_ready", "exp_ready", "h_ready", "h_out"))
        hT_done, hT_ready, logit_done, dlt_ready, edlt_ready = (sem(n) for n in ("hT_done", "hT_ready", "logit_done", "dlt_ready", "edlt_ready"))
        picks_ready, pre_done, load_ready, tab_done, rows_ready, bexp_ready = (sem(n) for n in ("picks_ready", "pre_done", "load_ready", "tab_done", "rows_ready", "bexp_ready"))
        sup_done, ssilu_ready, sact_ready, sdown_done, sum_ready, sum_out = (sem(n) for n in ("sup_done", "ssilu_ready", "sact_ready", "sdown_done", "sum_ready", "sum_out"))
        xg_in = [sem(f"xg_in{i}") for i in range(3)]
        xgT_done, xgT_ready, gate_done, up_done, silu_ready, act_ready, actT_done, actT_ready, y_done, y_ready, y_added = (
            sem(n) for n in ("xgT_done", "xgT_ready", "gate_done", "up_done", "silu_ready", "act_ready", "actT_done", "actT_ready", "y_done", "y_ready", "y_added"))

        block = ctx.enter_context(nc.Block())

        @block.sync
        def _(sp):
            sp.dma_start(ctx_sb[0:C, :], ctxT).then_inc(small_in, 16)
            sp.dma_start(wk_sb[0:C, :], wkT).then_inc(small_in, 16)
            sp.dma_start(wk_sb[C:C + 1, :], bk.rearrange("(a n) -> a n", a=1)).then_inc(small_in, 16)
            sp.dma_start(xT_sb[:, :, :], xT.rearrange("(k p) t -> p k t", p=P)).then_inc(xT_in, 16)
            sp.dma_start(x_sb[:, :, :], x_t).then_inc(x_in, 16)
            sp.dma_start(wg_sb[:, :, :], wg.rearrange("(k p) f -> p k f", p=P)).then_inc(sw_in, 16)
            sp.dma_start(wu_sb[:, :, :], wu.rearrange("(k p) f -> p k f", p=P)).then_inc(sw_in, 16)
            sp.dma_start(wd_sb[:, :, :], wd.rearrange("(c p) d -> p c d", p=P)).then_inc(sw_in, 16)
            for e in range(E):
                sp.dma_start(w1_sb[:, e, :, :], w1[e].rearrange("(k p) f -> p k f", p=P)).then_inc(w1_in, 16)
                sp.dma_start(w2_sb[:, e, :, :], w2[e].rearrange("(c p) d -> p c d", p=P)).then_inc(w2_in, 16)
            sp.wait_ge(consts, 1)
            sp.dma_start(h_dram[T:T + P, :], zeros[:, :]).then_inc(h_out, 16)
            sp.dma_start(out[T:T + P, :], zeros[:, :]).then_inc(sum_out, 16)
            for hf in range(2):
                sp.wait_ge(h_ready, hf + 1)
                sp.dma_start(h_t[:, hf * HT:(hf + 1) * HT, :], h_sb[:, hf * HT:(hf + 1) * HT, :]).then_inc(h_out, 16)
            for hf in range(2):
                sp.wait_ge(sum_ready, HT * (hf + 1))
                sp.dma_start(out_t[:, hf * HT:(hf + 1) * HT, :], x_sb[:, hf * HT:(hf + 1) * HT, :]).then_inc(sum_out, 16)
            sp.wait_ge(h_out, 48)
            sp.wait_ge(sum_out, 48)
            sp.wait_ge(y_added, 16 * NB)

        @block.gpsimd
        def _(pool):
            pool.memset(ctx_sb[C:C + 1, :], 1.0).then_inc(ones_row, 1)
            pool.wait_ge(ones_row, 1)
            pool.memset(zeros[:, :], 0.0)
            pool.memset(ident[:, :], 0.0)
            pool.memset(before[:, :], 1.0)
            pool.memset(upto[:, :, :], 1.0)
            pool.memset(ones[:, :], 1.0)
            pool.iota(iota_e[:, :], [[1, E]], base=0, channel_multiplier=0, allow_small_or_imprecise_dtypes=True)
            pool.iota(iota_b[:, :], [[1, NB]], base=0, channel_multiplier=0, allow_small_or_imprecise_dtypes=True)
            pool.iota(iota_j[:, :], [[1, P]], base=0, channel_multiplier=0, allow_small_or_imprecise_dtypes=True)
            pool.iota(row_of[:, :], [[1, 1]], base=0, channel_multiplier=1, allow_small_or_imprecise_dtypes=True)
            pool.iota(back_of[:, :], [[-P, NT]], base=T, channel_multiplier=-1, allow_small_or_imprecise_dtypes=True)
            pool.iota(steps[:, :, :], [[0, E], [P, NT]], base=0, channel_multiplier=0,
                      allow_small_or_imprecise_dtypes=True).then_inc(pool_step, 1)
            pool.wait_ge(pool_step, 1)
            pool.affine_select(out=ident[:, :], in_=ident[:, :], compare_op=ALU.not_equal, fill=1.0,
                               base=0, pattern=[[-1, P]], channel_multiplier=1)
            pool.affine_select(out=before[:, :], in_=before[:, :], compare_op=ALU.is_gt, fill=0.0,
                               base=0, pattern=[[1, P]], channel_multiplier=-1)
            pool.affine_select(out=upto[:, :, :], in_=upto[:, :, :], compare_op=ALU.is_ge, fill=0.0,
                               base=0, pattern=[[1, E], [-1, E]], channel_multiplier=0).then_inc(consts, 1)

            def gather(b):
                pool.indirect_dma_start(out=xg[b % 3][:, :], out_offset=None, in_=h_dram,
                                        in_offset=bass.IndirectOffsetOnAxis(ap=rows[:, b:b + 1], axis=0)
                                        ).then_inc(xg_in[b % 3], 16)

            pool.wait_ge(h_out, 48)
            pool.wait_ge(rows_ready, 1)
            for b in range(3):
                gather(b)
            pool.wait_ge(sum_out, 48)
            for b in range(NB):
                if b + 3 < NB:
                    pool.wait_ge(xgT_done, b + 1)
                    gather(b + 3)
                pool.wait_ge(y_ready, b + 1)
                if b:
                    pool.wait_ge(y_added, 16 * b)
                pool.indirect_dma_start(out=out, out_offset=bass.IndirectOffsetOnAxis(ap=rows[:, b:b + 1], axis=0),
                                        in_=ysb[b % 3][:, :], in_offset=None, compute_op=ALU.add).then_inc(y_added, 16)

        @block.vector
        def _(dve):
            steps_done = [0]

            def link(ins):
                steps_done[0] += 1
                ins.then_inc(dve_step, 1)
                dve.wait_ge(dve_step, steps_done[0])

            def rsqrt(to, v, a, b):
                y, p, q = r_y[:, a:b], r_p[:, a:b], r_q[:, a:b]
                link(dve.tensor_scalar(y.bitcast(i32), v.bitcast(i32), 1, None, ALU.logical_shift_right))
                link(dve.tensor_scalar(y.bitcast(i32), y.bitcast(i32), -1.0, MAGIC, ALU.mult, ALU.add))
                for n in range(3):
                    link(dve.tensor_tensor(p, y, y, ALU.mult))
                    link(dve.scalar_tensor_tensor(q, p, -0.5, v, ALU.mult, ALU.mult))
                    link(dve.scalar_tensor_tensor(to if n == 2 else y, q, 1.5, y, ALU.add, ALU.mult))

            dve.wait_ge(small_in, 48)
            link(dve.tensor_reduce(cmean[:, :], ctx_sb[0:C, :].rearrange("c (b j) -> c b j", b=NBATCH), AX.X, ALU.add))
            link(dve.tensor_scalar(cmean[:, :], cmean[:, :], -1.0 / TB, None, ALU.mult))
            for b in range(NBATCH):
                last = dve.tensor_scalar(ctxc_sb[:, b * TB:(b + 1) * TB], ctx_sb[0:C, b * TB:(b + 1) * TB],
                                         cmean[:, b:b + 1], None, ALU.add)
            last.then_inc(ctxc_ready, 1)
            dve.wait_ge(x_in, 16)
            for t in range(NT):
                last = dve.bn_stats(stats[:, t, :], x_sb[:, t, :])
            link(last)
            for t in range(NT):
                last = dve.bn_aggr(mvx[:, t, :], stats[:, t, :])
            link(last)
            link(dve.tensor_scalar(var[:, :], mvx[:, :, 1], LN_EPS, None, ALU.add))
            rsqrt(rx[:, :], var[:, :], 0, NT)
            link(dve.tensor_scalar(rx[:, :], rx[:, :], SCALE, None, ALU.mult))
            dve.wait_ge(kvc_done, 1)
            dve.tensor_copy(kvc_sb[:, :, :].rearrange("p t c -> p (t c)"), bank[2][:, :]).then_inc(kvc_ready, 1)
            dve.wait_ge(oT_done, 1)
            dve.tensor_copy(oT_sb[:, 0:512], bank[3][0:C, :]).then_inc(oT_ready, 1)
            dve.wait_ge(oT_done, 2)
            dve.tensor_copy(oT_sb[:, 512:1024], bank[4][0:C, :]).then_inc(oT_ready, 1)

            def sim_of(t):
                b = (5, 6, 0, 1)[t // 2]
                return bank[b][:, (t % 2) * D:(t % 2 + 1) * D]

            for hf in range(2):
                a, b = hf * HT, (hf + 1) * HT
                tiles = range(a, b)
                dve.wait_ge(sim_done, hf + 1)
                for t in tiles:
                    last = dve.bn_stats(stats[:, t, :], sim_of(t))
                link(last)
                for t in tiles:
                    last = dve.bn_aggr(mvs[:, t, :], stats[:, t, :])
                link(last)
                link(dve.tensor_tensor(var[:, a:b], rx[:, a:b], rx[:, a:b], ALU.mult))
                link(dve.tensor_tensor(var[:, a:b], var[:, a:b], mvs[:, a:b, 1], ALU.mult))
                link(dve.tensor_scalar(var[:, a:b], var[:, a:b], SIM_EPS, None, ALU.add))
                rsqrt(rs[:, a:b], var[:, a:b], a, b)
                link(dve.tensor_tensor(rs[:, a:b], rs[:, a:b], rx[:, a:b], ALU.mult))
                if hf:
                    dve.wait_ge(exp_ready, HT)
                for t in tiles:
                    last = dve.scalar_tensor_tensor(z_sb[:, t - a, :], sim_of(t), mvs[:, t, 0:1], gam_sb[:, :],
                                                    ALU.subtract, ALU.mult)
                last.then_inc(sim_read, 1)
                dve.wait_ge(sim_read, hf + 1)
                for t in tiles:
                    last = dve.scalar_tensor_tensor(z_sb[:, t - a, :], z_sb[:, t - a, :], rs[:, t:t + 1], bet_sb[:, :],
                                                    ALU.mult, ALU.add)
                link(last)
                dve.tensor_reduce(nmax[:, a:b], z_sb[:, :, :], AX.X, ALU.max, negate=True).then_inc(max_ready, 1)
                dve.wait_ge(exp_ready, HT * (hf + 1))
                link(dve.reciprocal(einv[:, a:b], esum[:, a:b]))
                dve.wait_ge(tanh_ready, 1)
                link(dve.tensor_scalar(einv[:, a:b], einv[:, a:b], tanhs[:, 0:1], None, ALU.mult))
                for t in tiles:
                    last = dve.scalar_tensor_tensor(x_sb[:, t, :], z_sb[:, t - a, :], einv[:, t:t + 1], x_sb[:, t, :],
                                                    ALU.mult, ALU.add)
                link(last)
                for t in tiles:
                    last = dve.bn_stats(stats[:, t, :], x_sb[:, t, :])
                link(last)
                for t in tiles:
                    last = dve.bn_aggr(mvh[:, t, :], stats[:, t, :])
                link(last)
                link(dve.tensor_scalar(var[:, a:b], mvh[:, a:b, 1], LN_EPS, None, ALU.add))
                rsqrt(rh[:, a:b], var[:, a:b], a, b)
                for t in tiles:
                    last = dve.tensor_scalar(h_sb[:, t, :], x_sb[:, t, :], mvh[:, t, 0:1], rh[:, t:t + 1],
                                             ALU.subtract, ALU.mult)
                last.then_inc(h_ready, 1)

            for hf in range(2):
                dve.wait_ge(logit_done, hf + 1)
                last = dve.tensor_copy(logit[:, hf * HT:(hf + 1) * HT, :].rearrange("p t e -> p (t e)"),
                                       bank[3 + hf][:, 0:HT * E])
            link(last)
            for t in range(NT):
                last = dve.max(top[:, t, :], logit[:, t, :])
            link(last)
            dve.tensor_tensor(dlt[:, :], top[:, :, 1], top[:, :, 0], ALU.subtract).then_inc(dlt_ready, 1)
            for t in range(NT):
                last = dve.max_index(topi[:, t, :], top[:, t, :], logit[:, t, :])
            link(last)
            link(dve.tensor_copy(idxf[:, :, :], topi[:, :, 0:TOPK].rearrange("p t k -> p k t")))
            dve.wait_ge(consts, 1)
            hot_f = hot_e[:, :, :, :].rearrange("p k t e -> p (k t) e")
            link(dve.tensor_tensor(hot_f, iota_e[:, :].unsqueeze(1).to_broadcast([P, TOPK * NT, E]),
                                   idxf[:, :, :].rearrange("p k t -> p (k t)").unsqueeze(2).to_broadcast([P, TOPK * NT, E]),
                                   ALU.is_equal))
            dve.memset(picks[:, NT, :], 0.0)
            dve.tensor_tensor(picks[:, 0:NT, :], hot_e[:, 0, :, :], hot_e[:, 1, :, :], ALU.add).then_inc(picks_ready, 1)
            dve.wait_ge(edlt_ready, 1)
            link(dve.tensor_scalar(score[:, 0, :], edlt[:, :], 1.0, None, ALU.add))
            link(dve.reciprocal(score[:, 0, :], score[:, 0, :]))
            link(dve.tensor_scalar(score[:, 0, :], score[:, 0, :], tanhs[:, 1:2], None, ALU.mult))
            link(dve.tensor_tensor(score[:, 1, :], score[:, 0, :], edlt[:, :], ALU.mult))
            dve.wait_ge(pre_done, 1)
            link(dve.tensor_copy(pre[:, :, :].rearrange("p t e -> p (t e)"), bank[5][:, 0:(NT + 1) * E]))
            link(dve.tensor_tensor(over[:, :, :], pre[:, NT, :].unsqueeze(2).to_broadcast([P, E, NT]), steps[:, :, :], ALU.is_gt))
            link(dve.tensor_reduce(nblk[:, :], over[:, :, :], AX.X, ALU.add))
            link(dve.tensor_tensor(cum[:, :, :], upto[:, :, :], nblk[:, :].unsqueeze(1).to_broadcast([P, E, E]), ALU.mult))
            link(dve.tensor_reduce(bend[:, :], cum[:, :, :], AX.X, ALU.add))
            link(dve.tensor_tensor(sstart[:, :], bend[:, :], nblk[:, :], ALU.subtract))
            link(dve.tensor_scalar(sstart[:, :], sstart[:, :], float(P), None, ALU.mult))
            link(dve.tensor_tensor(pre[:, 0:NT, :], pre[:, 0:NT, :], sstart[:, :].unsqueeze(1).to_broadcast([P, NT, E]), ALU.add))
            for k in range(TOPK):
                last = dve.tensor_tensor(slotp[:, k, :, :], hot_e[:, k, :, :], pre[:, 0:NT, :], ALU.mult)
            link(last)
            link(dve.tensor_reduce(slotf[:, :], slotp[:, :, :, :].rearrange("p k t e -> p (k t) e"), AX.X, ALU.add))
            link(dve.tensor_copy(sloti[:, :], slotf[:, :]))
            dve.tensor_scalar(posi[:, 0, :], sloti[:, :], P.bit_length() - 1, None, ALU.logical_shift_right)
            link(dve.tensor_scalar(posi[:, 1, :], sloti[:, :], P - 1, None, ALU.bitwise_and))
            link(dve.tensor_copy(posf[:, :, :], posi[:, :, :]))
            link(dve.tensor_tensor(hot_b[:, :, :], iota_b[:, :].unsqueeze(1).to_broadcast([P, TOPK * NT, NB]),
                                   posf[:, 0, :].unsqueeze(2).to_broadcast([P, TOPK * NT, NB]), ALU.is_equal))
            for k in range(TOPK):
                dve.tensor_tensor(load[:, k * NT:(k + 1) * NT, 0, :], hot_b[:, k * NT:(k + 1) * NT, :],
                                  back_of[:, :].unsqueeze(2).to_broadcast([P, NT, NB]), ALU.mult)
            dve.tensor_tensor(load[:, :, 1, :], hot_b[:, :, :],
                              score[:, :, :].rearrange("p k t -> p (k t)").unsqueeze(2).to_broadcast([P, TOPK * NT, NB]), ALU.mult)
            dve.tensor_tensor(hot_j[:, :, :], iota_j[:, :].unsqueeze(1).to_broadcast([P, TOPK * NT, P]),
                              posf[:, 1, :].unsqueeze(2).to_broadcast([P, TOPK * NT, P]), ALU.is_equal).then_inc(load_ready, 1)
            link(dve.tensor_tensor(bge[:, :, :], iota_b[:, :].unsqueeze(2).to_broadcast([P, NB, E]),
                                   bend[:, :].unsqueeze(1).to_broadcast([P, NB, E]), ALU.is_ge))
            link(dve.tensor_reduce(bexp[:, :], bge[:, :, :], AX.X, ALU.add))
            dve.tensor_scalar(bexpi[:, :], bexp[:, :], float(E - 1), None, ALU.min).then_inc(bexp_ready, 1)
            dve.wait_ge(tab_done, 1)
            link(dve.tensor_copy(tab[:, :, :].rearrange("p a b -> p (a b)"), bank[6][:, 0:2 * NB]))
            link(dve.tensor_scalar(padrow[:, :], tab[:, 0, :], 0.0, row_of[:, 0:1], ALU.is_equal, ALU.mult))
            link(dve.tensor_tensor(padrow[:, :], padrow[:, :], tab[:, 0, :], ALU.subtract))
            dve.tensor_scalar(rows[:, :], padrow[:, :], float(T), None, ALU.add).then_inc(rows_ready, 1)

            for hf in range(2):
                for c in range(SC):
                    n = hf * SC + c
                    dve.wait_ge(ssilu_ready, n + 1)
                    dve.tensor_tensor(saT[:, c, :], sg[:, :], bank[(2, 7)[n % 2]][:, :], ALU.mult).then_inc(sact_ready, 1)
                for t in range(HT):
                    n = hf * HT + t
                    dve.wait_ge(sdown_done, n + 1)
                    dve.scalar_tensor_tensor(x_sb[:, n, :], bank[3 + n % 2][:, 0:D], tanhs[:, 1:2], x_sb[:, n, :],
                                             ALU.mult, ALU.add).then_inc(sum_ready, 1)

            def actT_out(i):
                dve.wait_ge(actT_done, i + 1)
                dve.tensor_copy(actT[:, :], bank[6][:, :]).then_inc(actT_ready, 1)

            def act_out(i):
                dve.wait_ge(silu_ready, i + 1)
                dve.wait_ge(up_done, i + 1)
                dve.tensor_tensor(act[:, :], sg[:, :], bank[2][:, :], ALU.mult).then_inc(act_ready, 1)

            act_out(0)
            with dve.Fori(1, NB) as i:
                actT_out(i - 1)
                act_out(i)
            actT_out(NB - 1)

        @block.scalar
        def _(act_e):
            act_e.dma_start(gates[:, 0:1], g_att.partition_broadcast(P)).then_inc(act_step, 16)
            act_e.dma_start(gates[:, 1:2], g_ffn.partition_broadcast(P)).then_inc(act_step, 16)
            act_e.dma_start(gam_sb[:, :], gamma.partition_broadcast(P)).then_inc(act_step, 16)
            act_e.dma_start(bet_sb[:, :], beta.partition_broadcast(P)).then_inc(act_step, 16)
            act_e.dma_start(rw_sb[:, :, :], rw.rearrange("(k p) e -> p k e", p=P)).then_inc(act_step, 16)
            act_e.wait_ge(act_step, 80)
            act_e.activation(tanhs[:, :], gates[:, :], ACT.Tanh).then_inc(tanh_ready, 1)
            for n in range(2):
                act_e.wait_ge(kvT_done, n + 1)
                act_e.activation(kvT_sb[:, n * 512:(n + 1) * 512], bank[n][0:C, :], ACT.Copy).then_inc(kvT_ready, 1)
            for hf in range(2):
                act_e.wait_ge(max_ready, hf + 1)
                for t in range(hf * HT, (hf + 1) * HT):
                    act_e.activation(z_sb[:, t - hf * HT, :], z_sb[:, t - hf * HT, :], ACT.Exp, bias=nmax[:, t:t + 1],
                                     accum_out=esum[:, t:t + 1]).then_inc(exp_ready, 1)
                for k in range(KC):
                    act_e.wait_ge(hT_done, hf * KC + k + 1)
                    act_e.activation(hT_sb[:, k, hf * 512:(hf + 1) * 512], bank[(7, 2)[k]][:, :], ACT.Copy).then_inc(hT_ready, 1)
            act_e.wait_ge(dlt_ready, 1)
            act_e.activation(edlt[:, :], dlt[:, :], ACT.Exp).then_inc(edlt_ready, 1)
            for n in range(2 * SC):
                act_e.wait_ge(sup_done, n + 1)
                if n:
                    act_e.wait_ge(sact_ready, n)
                act_e.activation(sg[:, :], bank[n % 2][:, :], ACT.Silu).then_inc(ssilu_ready, 1)

            def xgT_out(i, s):
                act_e.wait_ge(xgT_done, i + 1)
                act_e.activation(xgT[s][:, :], bank[5][:, 0:D], ACT.Copy).then_inc(xgT_ready, 1)

            def silu(i):
                act_e.wait_ge(gate_done, i + 1)
                act_e.activation(sg[:, :], bank[0][:, :], ACT.Silu).then_inc(silu_ready, 1)

            def y_out(i, s, yslot_used):
                act_e.wait_ge(y_done, i + 1)
                if yslot_used is not None:
                    act_e.wait_ge(y_added, yslot_used)
                act_e.activation(ysb[s][:, :], bank[(3, 4, 7)[s]][:, 0:D], ACT.Copy,
                                 scale=tab[:, 1, bass.ds(i, 1)]).then_inc(y_ready, 1)

            xgT_out(0, 0)
            xgT_out(1, 1)
            silu(0)
            for i in range(1, 4):
                xgT_out(i + 1, (i + 1) % 3)
                silu(i)
                y_out(i - 1, (i - 1) % 3, None)
            with act_e.Fori(1, (NB - 2) // 3) as j:
                for u in range(3):
                    i = j * 3 + (u + 1)
                    xgT_out(i + 1, (u + 2) % 3)
                    silu(i)
                    y_out(i - 1, u, (i - 3) * 16)
            silu(NB - 1)
            y_out(NB - 2, (NB - 2) % 3, 16 * (NB - 4))
            y_out(NB - 1, (NB - 1) % 3, 16 * (NB - 3))

        @block.tensor
        def _(pe):
            pe.wait_ge(small_in, 48)
            pe.wait_ge(ones_row, 1)
            for n in range(2):
                pe.matmul(bank[n][0:C, :], wk_sb[:, :], ctx_sb[:, n * 512:(n + 1) * 512], start=True, stop=True).then_inc(kvT_done, 1)
            pe.wait_ge(ctxc_ready, 1)
            for t in range(NT):
                last = pe.matmul(bank[2][:, t * C:(t + 1) * C], ctxc_sb[:, t * P:(t + 1) * P], wk_sb[0:C, :], start=True, stop=True)
            last.then_inc(kvc_done, 1)
            pe.wait_ge(kvc_ready, 1)
            pe.wait_ge(xT_in, 16)
            for b in range(NBATCH):
                o = bank[3 + b // 2][0:C, (b % 2) * TB:(b % 2 + 1) * TB]
                for k in range(KC):
                    last = pe.matmul(o, kvc_sb[:, b * KC + k, :], xT_sb[:, k, b * TB:(b + 1) * TB], start=(k == 0), stop=(k == KC - 1))
                if b % 2:
                    last.then_inc(oT_done, 1)
            pe.wait_ge(kvT_ready, 2)
            for t in range(NT):
                if t % HT == 0:
                    pe.wait_ge(oT_ready, t // HT + 1)
                bk_ = bank[(5, 6, 0, 1)[t // 2]]
                b = t * P // TB
                last = pe.matmul(bk_[:, (t % 2) * D:(t % 2 + 1) * D], oT_sb[:, t * P:(t + 1) * P], kvT_sb[:, b * TB:(b + 1) * TB],
                                 start=True, stop=True)
                if t % HT == HT - 1:
                    last.then_inc(sim_done, 1)
            pe.wait_ge(consts, 1)
            for hf in range(2):
                pe.wait_ge(h_ready, hf + 1)
                if hf:
                    pe.wait_ge(hT_ready, KC)
                for k in range(KC):
                    for t in range(HT):
                        last = pe.transpose(bank[(7, 2)[k]][:, t * P:(t + 1) * P], h_sb[:, hf * HT + t, k * P:(k + 1) * P], ident[:, :])
                    last.then_inc(hT_done, 1)
                pe.wait_ge(hT_ready, KC * (hf + 1))
                for t in range(HT):
                    tt = hf * HT + t
                    for k in range(KC):
                        last = pe.matmul(bank[3 + hf][:, t * E:(t + 1) * E], hT_sb[:, k, tt * P:(tt + 1) * P], rw_sb[:, k, :],
                                         start=(k == 0), stop=(k == KC - 1))
                last.then_inc(logit_done, 1)
            pe.wait_ge(picks_ready, 1)
            NP = (NT + 1) * E
            pe.matmul(bank[5][:, 0:NP], before[:, :], picks[:, :, :].rearrange("p t e -> p (t e)"), start=True, stop=False)
            for t in range(NT):
                last = pe.matmul(bank[5][:, (t + 1) * E:NP].rearrange("p (t e) -> p t e", e=E), ones[:, :],
                                 picks[:, t:t + 1, :].to_broadcast([P, NT - t, E]), start=False, stop=(t == NT - 1))
            last.then_inc(pre_done, 1)
            pe.wait_ge(load_ready, 1)
            for n in range(TOPK * NT):
                last = pe.matmul(bank[6][:, 0:2 * NB], hot_j[:, n, :], load[:, n, :, :].rearrange("p a b -> p (a b)"),
                                 start=(n == 0), stop=(n == TOPK * NT - 1))
            last.then_inc(tab_done, 1)

            pe.wait_ge(sw_in, 48)
            for hf in range(2):
                for c in range(SC):
                    n = hf * SC + c
                    if n >= 2:
                        pe.wait_ge(sact_ready, n - 1)
                    for w, b in ((wg_sb, bank[n % 2]), (wu_sb, bank[(2, 7)[n % 2]])):
                        for k in range(KC):
                            last = pe.matmul(b[:, :], w[:, k, c * P:(c + 1) * P], hT_sb[:, k, hf * 512:(hf + 1) * 512],
                                             start=(k == 0), stop=(k == KC - 1))
                    last.then_inc(sup_done, 1)
                for t in range(HT):
                    n = hf * HT + t
                    if t == 0:
                        pe.wait_ge(sact_ready, SC * (hf + 1))
                    if n >= 2:
                        pe.wait_ge(sum_ready, n - 1)
                    for c in range(SC):
                        last = pe.matmul(bank[3 + n % 2][:, 0:D], saT[:, c, t * P:(t + 1) * P], wd_sb[:, c, :],
                                         start=(c == 0), stop=(c == SC - 1))
                    last.then_inc(sdown_done, 1)

            pe.wait_ge(w1_in, 16 * E)
            pe.wait_ge(w2_in, 16 * E)
            pe.wait_ge(bexp_ready, 1)
            pe.wait_ge(sum_ready, NT)

            def trans_x(i, s, count):
                pe.wait_ge(xg_in[s], count)
                pe.wait_ge(xgT_ready, i)
                for k in range(KC):
                    last = pe.transpose(bank[5][:, k * P:(k + 1) * P], xg[s][:, k * P:(k + 1) * P], ident[:, :])
                last.then_inc(xgT_done, 1)

            def up(i, s, e):
                pe.wait_ge(xgT_ready, i + 1)
                for half, b, done in ((0, bank[0], gate_done), (1, bank[2], up_done)):
                    for k in range(KC):
                        last = pe.matmul(b[:, :], xgT[s][:, k * P:(k + 1) * P],
                                         w1_sb[:, bass.ds(e, 1), k, half * F:(half + 1) * F].rearrange("p a f -> p (a f)"),
                                         start=(k == 0), stop=(k == KC - 1))
                    last.then_inc(done, 1)

            def trans_a(i):
                pe.wait_ge(act_ready, i + 1)
                for c in range(FC):
                    last = pe.transpose(bank[6][:, c * P:(c + 1) * P], act[:, c * P:(c + 1) * P], ident[:, :])
                last.then_inc(actT_done, 1)

            def down(i, s, e, free):
                pe.wait_ge(actT_ready, i + 1)
                if free is not None:
                    pe.wait_ge(y_ready, free)
                for c in range(FC):
                    last = pe.matmul(bank[(3, 4, 7)[s]][:, 0:D], actT[:, c * P:(c + 1) * P],
                                     w2_sb[:, bass.ds(e, 1), c, :].rearrange("p a d -> p (a d)"),
                                     start=(c == 0), stop=(c == FC - 1))
                last.then_inc(y_done, 1)

            def expert_of(i):
                return pe.value_load(bexpi[0:1, bass.ds(i, 1)], min_val=0, max_val=E - 1)

            pe.wait_ge(xg_in[0], 16)
            for k in range(KC):
                last = pe.transpose(bank[5][:, k * P:(k + 1) * P], xg[0][:, k * P:(k + 1) * P], ident[:, :])
            last.then_inc(xgT_done, 1)
            trans_x(1, 1, 16)
            up(0, 0, expert_of(0))
            for i in range(1, 4):
                trans_a(i - 1)
                trans_x(i + 1, (i + 1) % 3, 16 * ((i + 1) // 3 + 1))
                up(i, i % 3, expert_of(i))
                down(i - 1, (i - 1) % 3, expert_of(i - 1), None)
            with pe.Fori(1, (NB - 2) // 3) as j:
                for u in range(3):
                    i = j * 3 + (u + 1)
                    trans_a(i - 1)
                    trans_x(i + 1, (u + 2) % 3, (j + (1 if u == 0 else 2)) * 16)
                    up(i, (u + 1) % 3, expert_of(i))
                    down(i - 1, u, expert_of(i - 1), i - 3)
            i = NB - 1
            trans_a(i - 1)
            up(i, i % 3, expert_of(i))
            down(i - 1, (i - 1) % 3, expert_of(i - 1), i - 3)
            trans_a(i)
            down(i, i % 3, expert_of(i), i - 2)


_PAD = 128


def kernel(x, ctx_512, g_xattn, g_ffn, L0_xattn_W_k, L0_xattn_b_k, L0_xattn_ln_gamma, L0_xattn_ln_beta,
           L0_ffn_router_w, L0_ffn_w1, L0_ffn_w2, L0_ffn_w_gate, L0_ffn_w_up, L0_ffn_w_down):
    import numpy as np
    import concourse.bacc as bacc
    from concourse import mybir as mb
    from concourse.bass_utils import run_bass_kernel_spmd

    nc = bacc.Bacc("TRN2", target_bir_lowering=False, num_devices=1)
    B, S, D = x.shape
    x2 = np.ascontiguousarray(np.asarray(x).reshape(B * S, D))
    c2 = np.asarray(ctx_512).reshape(B * S, -1)
    ins = {
        "x": x2, "xT": x2.T, "ctxT": c2.T, "wkT": np.asarray(L0_xattn_W_k).T, "bk": L0_xattn_b_k,
        "gamma": L0_xattn_ln_gamma, "beta": L0_xattn_ln_beta, "g_att": g_xattn, "g_ffn": g_ffn,
        "rw": L0_ffn_router_w, "w1": L0_ffn_w1, "w2": L0_ffn_w2, "wg": L0_ffn_w_gate, "wu": L0_ffn_w_up, "wd": L0_ffn_w_down,
    }
    arrays, args = {}, []
    for name, a in ins.items():
        a = np.ascontiguousarray(a)
        arrays[f"in_{name}"] = a
        args.append(nc.dram_tensor(f"in_{name}", a.shape, mb.dt.from_np(a.dtype), kind="ExternalInput").ap())
    args.append(nc.dram_tensor("out_rows", (B * S + _PAD, D), mb.dt.float32, kind="ExternalOutput").ap())
    gated_attention_moe(nc, *args)
    r = run_bass_kernel_spmd(nc, [arrays], core_ids=[0])
    return r.results[0]["out_rows"][0:B * S].reshape(B, S, D)
```

```python
import concourse.bass as bass
from concourse import mybir
from contextlib import ExitStack


def gated_attention_moe(nc, x, xT, ctxT, wkT, bk, gamma, beta, g_att, g_ffn, rw, w1, w2, wg, wu, wd, out):
    f32 = mybir.dt.float32
    i32 = mybir.dt.int32
    u32 = mybir.dt.uint32
    f16 = mybir.dt.float16
    bf16 = mybir.dt.bfloat16
    ALU = mybir.AluOpType
    ACT = mybir.ActivationFunctionType
    AX = mybir.AxisListType

    P = 128
    T, D = x.shape
    NT = T // P
    HT = NT // 2
    KC = D // P
    C = ctxT.shape[0]
    NBATCH = 4
    TB = T // NBATCH
    E = rw.shape[1]
    TOPK = 2
    F2 = w1.shape[2]
    F = F2 // 2
    FC = F // P
    SI = wg.shape[1]
    SC = SI // P
    NB = (TOPK * T + E * (P - 1)) // P
    SCALE = float(D) ** -0.5
    LN_EPS, SIM_EPS = 1e-5, 1e-6
    MAGIC = float(0x5F3759DF)

    H_SCALE = 2.0 ** 11
    LOW = 2.0 ** 11
    EXP = float(2 ** 23)

    x_t = x.rearrange("(t p) d -> p t d", p=P)
    out_t = out[0:T, :].rearrange("(t p) d -> p t d", p=P)
    h_dram = nc.dram_tensor("h_rows", (T + P, D), f32).ap()
    h_t = h_dram[0:T, :].rearrange("(t p) d -> p t d", p=P)

    ctx = ExitStack()
    with ctx:
        def sb(name, shape, dt=f32):
            return ctx.enter_context(nc.sbuf_tensor(name, shape, dt))

        def sem(name):
            return ctx.enter_context(nc.semaphore(name))

        bank = [ctx.enter_context(nc.psum_tensor(f"bank{i}", [P, 512], f32)) for i in range(8)]

        x_sb = sb("x_sb", [P, NT, D])
        xT_sb = sb("xT_sb", [P, KC, T])
        h_sb = xT_sb[:, :, :].rearrange("p k (a d) -> p (k a) d", d=D)
        early = sb("early", [P, 4, T])
        ctx_sb, ctxc_sb, kvT_sb, oT_sb = early[0:C + 1, 0, :], early[0:C, 1, :], early[0:C, 2, :], early[0:C, 3, :]
        saT = early[:, :, :].rearrange("p a (b n) -> p (a b) n", n=512)
        wk_sb = sb("wk_sb", [C + 1, C])
        gambet = sb("gambet", [P, 2 * D])
        gam_sb, bet_sb = gambet[:, 0:D], gambet[:, D:2 * D]
        gates = sb("gates", [P, 2])
        tanhs = sb("tanhs", [P, 2])
        rw_sb = sb("rw_sb", [P, KC, E])
        wsh = sb("wsh", [P, 2, KC, SI], f16)
        wsl = sb("wsl", [P, 2, KC, SI], f16)
        wd_sb = sb("wd_sb", [P, SC, D])
        N1, N2 = KC * F2, FC * D
        stage = sb("stage", [P, 2, N1 + N2])
        w1h = sb("w1h", [P, E, KC, F2], f16)
        w1l = sb("w1l", [P, E, KC, F2], f16)
        w2h = sb("w2h", [P, E, FC, D], f16)
        w2l = sb("w2l", [P, E, FC, D], f16)
        NS = KC * SI
        raws = w1l[:, E // 2:, :, :].rearrange("p e k f -> p (e k f)").bitcast(f32)
        warm = sb("warm", [P, 2 * D], bf16)
        zeros = warm[:, :].bitcast(f32)
        ident = sb("ident", [P, P])
        before = sb("before", [P, P], bf16)
        ones = sb("ones", [P, P])
        ones_b = sb("ones_b", [P, P], bf16)
        iota_e = sb("iota_e", [P, E])
        iota_b = sb("iota_b", [P, NB])
        iota_j = sb("iota_j", [P, P])
        row_of = sb("row_of", [P, 1])
        back_of = sb("back_of", [P, NT])
        steps = sb("steps", [P, E, NT])
        upto = sb("upto", [P, E, E])
        cmean = sb("cmean", [C, NBATCH])
        kvc_sb = sb("kvc_sb", [P, NT, C])
        stats = sb("stats", [P, NT, 6])
        mvx = sb("mvx", [P, NT, 2])
        mvs = sb("mvs", [P, NT, 2])
        mvh = sb("mvh", [P, NT, 2])
        var = sb("var", [P, NT])
        r_y = sb("r_y", [P, NT])
        r_p = sb("r_p", [P, NT])
        r_q = sb("r_q", [P, NT])
        rx = sb("rx", [P, NT])
        rs = sb("rs", [P, NT])
        rh = sb("rh", [P, NT])
        offh = sb("offh", [P, NT])
        nmax = sb("nmax", [P, NT])
        esum = sb("esum", [P, NT])
        einv = sb("einv", [P, NT])
        mid = sb("mid", [P, NT, D])
        z_sb = mid[:, :, :]
        hT32 = [mid[:, i * HT:(i + 1) * HT, :].rearrange("p t d -> p (t d)").rearrange("p (k n) -> p k n", k=KC) for i in range(2)]
        hot_j = mid[:, :, :].rearrange("p t (a j) -> p (t a) j", j=P)
        hTh = sb("hTh", [P, KC, T], f16)
        hTl = sb("hTl", [P, KC, T], f16)
        spare = xT_sb[:, :, :].rearrange("p k t -> p (k t)")
        load = spare[:, 0:TOPK * NT * 2 * NB].rearrange("p (n a b) -> p n a b", a=2, b=NB)
        spare = spare[:, TOPK * NT * 2 * NB:]
        hot_b = spare[:, 0:TOPK * NT * NB].rearrange("p (n b) -> p n b", b=NB)
        spare = spare[:, TOPK * NT * NB:]
        bge = spare[:, 0:NB * E].rearrange("p (b e) -> p b e", e=E)
        bnm = spare[:, NB * E:2 * NB * E].rearrange("p (b e) -> p b e", e=E)
        act = spare[:, 2 * NB * E:2 * NB * E + F]
        logit = sb("logit", [P, NT, E])
        top = sb("top", [P, NT, 8])
        topi = sb("topi", [P, NT, 8], u32)
        idxf = sb("idxf", [P, TOPK, NT])
        hot_e = sb("hot_e", [P, TOPK, NT, E])
        picks = sb("picks", [P, NT + 1, E], bf16)
        dlt = sb("dlt", [P, NT])
        edlt = sb("edlt", [P, NT])
        score = sb("score", [P, TOPK, NT])
        pre = sb("pre", [P, NT + 1, E])
        over = sb("over", [P, E, NT])
        nblk = sb("nblk", [P, E])
        cum = sb("cum", [P, E, E])
        bend = sb("bend", [P, E])
        sstart = sb("sstart", [P, E])
        slotp = sb("slotp", [P, TOPK, NT, E])
        slotf = sb("slotf", [P, TOPK * NT])
        sloti = sb("sloti", [P, TOPK * NT], i32)
        posi = sb("posi", [P, 2, TOPK * NT], i32)
        posf = sb("posf", [P, 2, TOPK * NT])
        tab = sb("tab", [P, 2, NB])
        padrow = sb("padrow", [P, NB])
        rows = sb("rows", [P, NB], i32)
        bexp = sb("bexp", [P, NB])
        bexpi = sb("bexpi", [P, NB], i32)
        sumsq_s = sb("sumsq_s", [P, 2])
        nexp_s = sb("nexp_s", [P, 2], i32)
        wscale_s = sb("wscale_s", [P, 2])
        up_f = sb("up_f", [P, 2])
        sumsq = sb("sumsq", [P, 2, E])
        nexp_i = sb("nexp_i", [P, 2, E], i32)
        nexp = sb("nexp", [P, 2, E])
        wscale = sb("wscale", [P, 2, E])
        bnx = sb("bnx", [P, 2, NB])
        silu_f = sb("silu_f", [P, NB])
        act_f = sb("act_f", [P, NB])
        y_x = sb("y_x", [P, NB])
        y_f = sb("y_f", [P, NB])
        y_fl = sb("y_fl", [P, NB])
        sg = sb("sg", [P, 512])[:, :]
        sgs = (sg, gambet[:, :])
        flat = mid[:, :, :].rearrange("p t d -> p (t d)")
        xg = [flat[:, i * D:(i + 1) * D] for i in range(3)]
        half = flat[:, 3 * D:6 * D].bitcast(f16)
        xTh = [half[:, (2 * i) * D:(2 * i + 1) * D] for i in range(3)]
        xTl = [half[:, (2 * i + 1) * D:(2 * i + 2) * D] for i in range(3)]
        flat = stage[:, :, :].rearrange("p a n -> p (a n)")
        ysb = [flat[:, i * D:(i + 1) * D] for i in range(3)]
        yhi = [flat[:, (3 + i) * D:(4 + i) * D] for i in range(3)]
        half = flat[:, 6 * D:8 * D].bitcast(f16)
        aTh, aTl = half[:, 0:2 * D], half[:, 2 * D:4 * D]

        ctx_in, wk_in, gate_in, x_in, xT_in, wg_in, wu_in, down_in = (
            sem(n) for n in ("ctx_in", "wk_in", "gate_in", "x_in", "xT_in", "wg_in", "wu_in", "down_in"))
        raw1_in = [sem(f"raw1_in{i}") for i in range(2)]
        raw2_in = [sem(f"raw2_in{i}") for i in range(2)]
        consts, pool_step, ones_row, warm_ready = sem("consts"), sem("pool_step"), sem("ones_row"), sem("warm_ready")
        dve_step = sem("dve_step")
        ctxc_ready, kvT_done, kvc_done, kvT_ready, kvc_ready = (sem(n) for n in ("ctxc_ready", "kvT_done", "kvc_done", "kvT_ready", "kvc_ready"))
        oT_done, oT_ready, sim_done, rs_ready, zc_ready, zn_ready = (sem(n) for n in ("oT_done", "oT_ready", "sim_done", "rs_ready", "zc_ready", "zn_ready"))
        x1_ready = sem("x1_ready")
        tanh_ready, max_ready, exp_ready, rh_ready, h_ready, h_out = (sem(n) for n in ("tanh_ready", "max_ready", "exp_ready", "rh_ready", "h_ready", "h_out"))
        hT_done, hT_ready, logit_done, dlt_ready, edlt_ready = (sem(n) for n in ("hT_done", "hT_ready", "logit_done", "dlt_ready", "edlt_ready"))
        picks_ready, pre_done, load_ready, tab_done, rows_ready, factors_ready = (sem(n) for n in ("picks_ready", "pre_done", "load_ready", "tab_done", "rows_ready", "factors_ready"))
        sup_done, ssilu_ready, sact_ready, sdown_done, sum_ready, sum_out = (sem(n) for n in ("sup_done", "ssilu_ready", "sact_ready", "sdown_done", "sum_ready", "sum_out"))
        sq1_ready, norm1_done, scale1_ready, high1_ready, low1_ready = (sem(n) for n in ("sq1_ready", "norm1_done", "scale1_ready", "high1_ready", "low1_ready"))
        sq2_ready, norm2_done, scale2_ready, high2_ready, low2_ready = (sem(n) for n in ("sq2_ready", "norm2_done", "scale2_ready", "high2_ready", "low2_ready"))
        scaled2_ready = sem("scaled2_ready")
        sqs_ready, norms_done, scales_ready, scaleds_ready, highs_ready, lows_ready = (
            sem(n) for n in ("sqs_ready", "norms_done", "scales_ready", "scaleds_ready", "highs_ready", "lows_ready"))
        hTh_ready, hTl_ready = sem("hTh_ready"), sem("hTl_ready")
        xg_in = [sem(f"xg_in{i}") for i in range(3)]
        xT_done, xh_ready, xl_ready, gate_done, up_done, silu_ready, act_ready = (
            sem(n) for n in ("xgT_done", "xh_ready", "xl_ready", "gate_done", "up_done", "silu_ready", "act_ready"))
        aT_done, ah_ready, al_ready, y_done, yhi_ready, y_ready, y_added = (
            sem(n) for n in ("aT_done", "ah_ready", "al_ready", "y_done", "yhi_ready", "y_ready", "y_added"))

        SIM_BANK = (0, 1, 5, 7)
        G_BANK, U_BANK, Y_BANK = (0, 1), (2, 7), (3, 4)
        YB_BANK = (3, 4, 7)

        def sim_of(t):
            return bank[SIM_BANK[t // 2]][:, (t % 2) * D:(t % 2 + 1) * D]

        SLOTS = []
        for hf in range(2):
            SLOTS += [("up", hf, c) for c in range(SC)] + [("down", hf, t) for t in range(HT)]

        BASE = (2, 5, 8, 10, 12, 15, 18, 21)

        def prepare(k, *what):
            for lead, step in what:
                for e in range(E):
                    if BASE[e] - lead == k:
                        step(e)

        block = ctx.enter_context(nc.Block())

        @block.sync
        def _(sp):
            def raw1(e):
                sp.dma_start(stage[:, e % 2, 0:N1].rearrange("p (k f) -> p k f", k=KC),
                             w1[e].rearrange("(k p) f -> p k f", p=P)).then_inc(raw1_in[e % 2], 16)

            def raw2(e):
                sp.dma_start(stage[:, e % 2, N1:].rearrange("p (c d) -> p c d", c=FC),
                             w2[e].rearrange("(c p) d -> p c d", p=P)).then_inc(raw2_in[e % 2], 16)

            sp.dma_start(ctx_sb[0:C, :], ctxT).then_inc(ctx_in, 16)
            sp.dma_start(wk_sb[0:C, :], wkT).then_inc(wk_in, 16)
            sp.dma_start(wk_sb[C:C + 1, :], bk.rearrange("(a n) -> a n", a=1)).then_inc(wk_in, 16)
            sp.dma_start(x_sb[:, :, :], x_t).then_inc(x_in, 16)
            sp.dma_start(xT_sb[:, :, :], xT.rearrange("(k p) t -> p k t", p=P)).then_inc(xT_in, 16)
            sp.dma_start(gates[:, 0:1], g_att.partition_broadcast(P)).then_inc(gate_in, 16)
            sp.dma_start(gates[:, 1:2], g_ffn.partition_broadcast(P)).then_inc(gate_in, 16)
            sp.dma_start(gam_sb, gamma.partition_broadcast(P)).then_inc(gate_in, 16)
            sp.dma_start(bet_sb, beta.partition_broadcast(P)).then_inc(gate_in, 16)
            sp.dma_start(rw_sb[:, :, :], rw.rearrange("(k p) e -> p k e", p=P)).then_inc(gate_in, 16)
            sp.dma_start(raws[:, 0:NS].rearrange("p (k f) -> p k f", k=KC), wg.rearrange("(k p) f -> p k f", p=P)).then_inc(wg_in, 16)
            sp.dma_start(raws[:, NS:].rearrange("p (k f) -> p k f", k=KC), wu.rearrange("(k p) f -> p k f", p=P)).then_inc(wu_in, 16)
            raw1(0)
            raw2(0)
            raw1(1)
            raw2(1)
            sp.dma_start(wd_sb[:, :, :], wd.rearrange("(c p) d -> p c d", p=P)).then_inc(down_in, 16)
            sp.wait_ge(warm_ready, 1)
            sp.dma_start(h_dram[T:T + P, :], zeros).then_inc(h_out, 16)
            sp.dma_start(out[T:T + P, :], zeros).then_inc(sum_out, 16)
            for hf in range(2):
                sp.wait_ge(h_ready, HT * (hf + 1))
                sp.dma_start(h_t[:, hf * HT:(hf + 1) * HT, :], h_sb[:, hf * HT:(hf + 1) * HT, :]).then_inc(h_out, 16)
            for e in range(2, E):
                sp.wait_ge(low1_ready, e - 1)
                raw1(e)
                sp.wait_ge(low2_ready, e - 1)
                raw2(e)
            for hf in range(2):
                sp.wait_ge(sum_ready, HT * (hf + 1))
                sp.dma_start(out_t[:, hf * HT:(hf + 1) * HT, :], x_sb[:, hf * HT:(hf + 1) * HT, :]).then_inc(sum_out, 16)
            sp.wait_ge(h_out, 48)
            sp.wait_ge(sum_out, 48)
            sp.wait_ge(y_added, 16 * NB)

        @block.gpsimd
        def _(pool):
            pool.memset(ctx_sb[C:C + 1, :], 1.0).then_inc(ones_row, 1)
            pool.wait_ge(ones_row, 1)
            pool.memset(ident[:, :], 0.0)
            pool.memset(before[:, :], 1.0)
            pool.memset(upto[:, :, :], 1.0)
            pool.memset(ones[:, :], 1.0)
            pool.memset(ones_b[:, :], 1.0)
            pool.iota(iota_e[:, :], [[1, E]], base=0, channel_multiplier=0, allow_small_or_imprecise_dtypes=True)
            pool.iota(iota_b[:, :], [[1, NB]], base=0, channel_multiplier=0, allow_small_or_imprecise_dtypes=True)
            pool.iota(iota_j[:, :], [[1, P]], base=0, channel_multiplier=0, allow_small_or_imprecise_dtypes=True)
            pool.iota(row_of[:, :], [[1, 1]], base=0, channel_multiplier=1, allow_small_or_imprecise_dtypes=True)
            pool.iota(back_of[:, :], [[-P, NT]], base=T, channel_multiplier=-1, allow_small_or_imprecise_dtypes=True)
            pool.iota(steps[:, :, :], [[0, E], [P, NT]], base=0, channel_multiplier=0,
                      allow_small_or_imprecise_dtypes=True).then_inc(pool_step, 1)
            pool.wait_ge(pool_step, 1)
            pool.affine_select(out=ident[:, :], in_=ident[:, :], compare_op=ALU.not_equal, fill=1.0,
                               base=0, pattern=[[-1, P]], channel_multiplier=1)
            pool.affine_select(out=before[:, :], in_=before[:, :], compare_op=ALU.is_gt, fill=0.0,
                               base=0, pattern=[[1, P]], channel_multiplier=-1)
            pool.affine_select(out=upto[:, :, :], in_=upto[:, :, :], compare_op=ALU.is_ge, fill=0.0,
                               base=0, pattern=[[1, E], [-1, E]], channel_multiplier=0).then_inc(consts, 1)
            def wide(scale, n):
                return scale.to_broadcast([P, n])

            for m in range(2):
                pool.wait_ge(scales_ready, m + 1)
                pool.tensor_tensor(raws[:, m * NS:(m + 1) * NS], raws[:, m * NS:(m + 1) * NS], wide(wscale_s[:, m:m + 1], NS),
                                   ALU.mult).then_inc(scaleds_ready, 1)
            for m in range(2):
                pool.wait_ge(highs_ready, m + 1)
                pool.tensor_tensor(wsl[:, m, :, :].rearrange("p k f -> p (k f)"), raws[:, m * NS:(m + 1) * NS],
                                   wsh[:, m, :, :].rearrange("p k f -> p (k f)"), ALU.subtract).then_inc(lows_ready, 1)

            def gather(b):
                pool.indirect_dma_start(out=xg[b % 3], out_offset=None, in_=h_dram,
                                        in_offset=bass.IndirectOffsetOnAxis(ap=rows[:, b:b + 1], axis=0)
                                        ).then_inc(xg_in[b % 3], 16)

            for e in range(E):
                pool.wait_ge(scale2_ready, e + 1)
                pool.tensor_tensor(stage[:, e % 2, N1:], stage[:, e % 2, N1:], wide(wscale[:, 1, e:e + 1], N2), ALU.mult).then_inc(scaled2_ready, 1)
                pool.wait_ge(high2_ready, e + 1)
                pool.tensor_tensor(w2l[:, e, :, :].rearrange("p c d -> p (c d)"), stage[:, e % 2, N1:],
                                   w2h[:, e, :, :].rearrange("p c d -> p (c d)"), ALU.subtract).then_inc(low2_ready, 1)
                if e == E - 3:
                    pool.wait_ge(h_out, 48)
                    pool.wait_ge(rows_ready, 1)
                    for b in range(3):
                        gather(b)
            pool.wait_ge(xT_done, 1)
            gather(3)
            pool.wait_ge(sum_out, 48)
            for b in range(NB):
                if b + 4 < NB:
                    pool.wait_ge(xT_done, b + 2)
                    gather(b + 4)
                pool.wait_ge(y_ready, b + 1)
                if b:
                    pool.wait_ge(y_added, 16 * b)
                pool.indirect_dma_start(out=out, out_offset=bass.IndirectOffsetOnAxis(ap=rows[:, b:b + 1], axis=0),
                                        in_=ysb[b % 3], in_offset=None, compute_op=ALU.add).then_inc(y_added, 16)

        @block.vector
        def _(dve):
            steps_done = [0]

            def link(ins, between=()):
                steps_done[0] += 1
                ins.then_inc(dve_step, 1)
                if between:
                    between.pop(0)()
                dve.wait_ge(dve_step, steps_done[0])

            def mark(ins):
                steps_done[0] += 1
                ins.then_inc(dve_step, 1)

            def rsqrt(to, v, a, b, between=()):
                y, p, q = r_y[:, a:b], r_p[:, a:b], r_q[:, a:b]
                link(dve.tensor_scalar(y.bitcast(i32), v.bitcast(i32), 1, None, ALU.logical_shift_right), between)
                link(dve.tensor_scalar(y.bitcast(i32), y.bitcast(i32), -1.0, MAGIC, ALU.mult, ALU.add), between)
                for n in range(3):
                    link(dve.tensor_tensor(p, y, y, ALU.mult), between)
                    link(dve.scalar_tensor_tensor(q, p, -0.5, v, ALU.mult, ALU.mult), between)
                    link(dve.scalar_tensor_tensor(to if n == 2 else y, q, 1.5, y, ALU.add, ALU.mult), between)

            def scale_of(e, m, norm_done, scale_ready):
                dve.wait_ge(norm_done, e + 1)
                link(dve.tensor_scalar(nexp_i[:, m, e:e + 1], bank[6][:, m * E + e:m * E + e + 1].bitcast(i32), 24, None, ALU.logical_shift_right))
                dve.tensor_copy(nexp[:, m, e:e + 1], nexp_i[:, m, e:e + 1])
                dve.tensor_scalar(wscale[:, m, e:e + 1].bitcast(i32), nexp_i[:, m, e:e + 1], -EXP, 204.0 * EXP,
                                  ALU.mult, ALU.add).then_inc(scale_ready, 1)

            def scale1_of(e):
                scale_of(e, 0, norm1_done, scale1_ready)

            def scale2_of(e):
                scale_of(e, 1, norm2_done, scale2_ready)

            def low1_of(e):
                dve.wait_ge(high1_ready, e + 1)
                dve.scalar_tensor_tensor(w1l[:, e, :, :].rearrange("p k f -> p (k f)"), stage[:, e % 2, 0:N1], wscale[:, 0, e:e + 1],
                                         w1h[:, e, :, :].rearrange("p k f -> p (k f)"), ALU.mult, ALU.subtract).then_inc(low1_ready, 1)

            def high2_of(e):
                dve.wait_ge(scaled2_ready, e + 1)
                dve.tensor_copy(w2h[:, e, :, :].rearrange("p c d -> p (c d)"), stage[:, e % 2, N1:]).then_inc(high2_ready, 1)

            def shared_exponent(m):
                def run():
                    dve.wait_ge(norms_done, m + 1)
                    mark(dve.tensor_scalar(nexp_s[:, m:m + 1], bank[6][:, 2 * E + m:2 * E + m + 1].bitcast(i32), 24, None, ALU.logical_shift_right))
                return run

            def shared_scale(m):
                def run():
                    dve.tensor_scalar(wscale_s[:, m:m + 1].bitcast(i32), nexp_s[:, m:m + 1], -EXP, 204.0 * EXP, ALU.mult, ALU.add).then_inc(scales_ready, 1)
                    dve.tensor_scalar(up_f[:, m:m + 1].bitcast(i32), nexp_s[:, m:m + 1], 39.0, EXP, ALU.add, ALU.mult)
                return run

            dve.memset(warm[:, :], 0.0).then_inc(warm_ready, 1)
            dve.wait_ge(ctx_in, 16)
            link(dve.tensor_reduce(cmean[:, :], ctx_sb[0:C, :].rearrange("c (b j) -> c b j", b=NBATCH), AX.X, ALU.add))
            link(dve.tensor_scalar(cmean[:, :], cmean[:, :], -1.0 / TB, None, ALU.mult))
            for b in range(NBATCH):
                last = dve.tensor_scalar(ctxc_sb[:, b * TB:(b + 1) * TB], ctx_sb[0:C, b * TB:(b + 1) * TB],
                                         cmean[:, b:b + 1], None, ALU.add)
            last.then_inc(ctxc_ready, 1)
            dve.wait_ge(x_in, 16)
            for t in range(NT):
                last = dve.bn_stats(stats[:, t, :], x_sb[:, t, :])
            link(last)
            for t in range(NT):
                last = dve.bn_aggr(mvx[:, t, :], stats[:, t, :])
            link(last)
            link(dve.tensor_scalar(var[:, :], mvx[:, :, 1], LN_EPS, None, ALU.add))
            rsqrt(rx[:, :], var[:, :], 0, NT)
            link(dve.tensor_scalar(rx[:, :], rx[:, :], SCALE, None, ALU.mult))
            def sim_stats(t):
                def run():
                    if t % 2 == 0:
                        dve.wait_ge(sim_done, t // 2 + 1)
                    mark(dve.bn_stats(stats[:, t, :], sim_of(t)))
                return run

            def centred(t):
                return lambda: dve.scalar_tensor_tensor(z_sb[:, t, :], sim_of(t), mvs[:, t, 0:1], gam_sb,
                                                        ALU.subtract, ALU.mult).then_inc(zc_ready, 1)

            def sim_factor(a, b, between):
                for t in range(a, b):
                    last = dve.bn_aggr(mvs[:, t, :], stats[:, t, :])
                link(last)
                link(dve.tensor_tensor(var[:, a:b], rx[:, a:b], rx[:, a:b], ALU.mult), between)
                link(dve.tensor_tensor(var[:, a:b], var[:, a:b], mvs[:, a:b, 1], ALU.mult), between)
                link(dve.tensor_scalar(var[:, a:b], var[:, a:b], SIM_EPS, None, ALU.add), between)
                rsqrt(rs[:, a:b], var[:, a:b], a, b, between)
                dve.scalar_tensor_tensor(rs[:, a:b], rs[:, a:b], -1.0, rx[:, a:b], ALU.mult, ALU.mult).then_inc(rs_ready, 1)

            def largest(t):
                def run():
                    dve.wait_ge(zn_ready, t + 1)
                    dve.tensor_tensor_reduce(out=z_sb[:, t, :], in0=z_sb[:, t, :], in1=bet_sb, scale=1.0, scalar=3.0e38,
                                             op0=ALU.add, op1=ALU.min, accum_out=nmax[:, t:t + 1]).then_inc(max_ready, 1)
                return run

            def weights(a, b, between=()):
                dve.wait_ge(exp_ready, b)
                link(dve.reciprocal(einv[:, a:b], esum[:, a:b]), between)
                link(dve.tensor_scalar(einv[:, a:b], einv[:, a:b], tanhs[:, 0:1], None, ALU.mult), between)

            def attended(t):
                return lambda: dve.scalar_tensor_tensor(x_sb[:, t, :], z_sb[:, t, :], einv[:, t:t + 1], x_sb[:, t, :],
                                                        ALU.mult, ALU.add).then_inc(x1_ready, 1)

            def stats_of(t):
                def run():
                    dve.wait_ge(x1_ready, t + 1)
                    mark(dve.bn_stats(stats[:, t, :], x_sb[:, t, :]))
                return run

            def norm_factor(a, b, between):
                for t in range(a, b):
                    last = dve.bn_aggr(mvh[:, t, :], stats[:, t, :])
                link(last)
                link(dve.tensor_scalar(var[:, a:b], mvh[:, a:b, 1], LN_EPS, None, ALU.add), between)
                rsqrt(rh[:, a:b], var[:, a:b], a, b, between)
                dve.scalar_tensor_tensor(offh[:, a:b], rh[:, a:b], -1.0, mvh[:, a:b, 0], ALU.mult, ALU.mult).then_inc(rh_ready, 1)

            def settle():
                dve.wait_ge(dve_step, steps_done[0])

            dve.wait_ge(gate_in, 80)
            link(dve.tensor_scalar(bet_sb, bet_sb, -1.0, None, ALU.mult))
            for t in range(HT):
                sim_stats(t)()
            shared_exponent(0)()
            settle()
            shared_scale(0)()
            between = [centred(t) for t in range(HT)] + [sim_stats(t) for t in range(HT, NT)] + [shared_exponent(1), shared_scale(1)]
            sim_factor(0, HT, between)
            assert not between
            settle()
            between = [centred(t) for t in range(HT, NT)] + [largest(t) for t in range(HT)]
            sim_factor(HT, NT, between)
            assert not between
            weights(0, HT)
            for t in range(HT):
                attended(t)()
            for t in range(HT):
                stats_of(t)()
            settle()
            between = [largest(t) for t in range(HT, NT)]
            norm_factor(0, HT, between)
            assert not between
            weights(HT, NT)
            for t in range(HT, NT):
                attended(t)()

            def hT_low(hf):
                for k in range(KC):
                    dve.wait_ge(hTh_ready, hf * KC + k + 1)
                    dve.scalar_tensor_tensor(hTl[:, k, hf * 512:(hf + 1) * 512], bank[(5, 4)[k]][:, :], H_SCALE,
                                             hTh[:, k, hf * 512:(hf + 1) * 512], ALU.mult, ALU.subtract).then_inc(hTl_ready, 1)

            for t in range(HT, NT):
                stats_of(t)()
            settle()
            hT_low(0)
            norm_factor(HT, NT, [])

            def top_two():
                dve.wait_ge(logit_done, 2)
                link(dve.tensor_copy(logit[:, :, :].rearrange("p t e -> p (t e)"), bank[3][:, 0:NT * E]))
                for t in range(NT):
                    last = dve.max(top[:, t, :], logit[:, t, :])
                link(last)
                dve.tensor_tensor(dlt[:, :], top[:, :, 1], top[:, :, 0], ALU.subtract).then_inc(dlt_ready, 1)

            def pick():
                for t in range(NT):
                    last = dve.max_index(topi[:, t, :], top[:, t, :], logit[:, t, :])
                link(last)
                link(dve.tensor_copy(idxf[:, :, :], topi[:, :, 0:TOPK].rearrange("p t k -> p k t")))
                link(dve.tensor_tensor(hot_e[:, :, :, :].rearrange("p k t e -> p (k t) e"),
                                       iota_e[:, :].unsqueeze(1).to_broadcast([P, TOPK * NT, E]),
                                       idxf[:, :, :].rearrange("p k t -> p (k t)").unsqueeze(2).to_broadcast([P, TOPK * NT, E]),
                                       ALU.is_equal))
                dve.memset(picks[:, NT, :], 0.0)
                dve.tensor_tensor(picks[:, 0:NT, :], hot_e[:, 0, :, :], hot_e[:, 1, :, :], ALU.add).then_inc(picks_ready, 1)

            def scores():
                dve.wait_ge(edlt_ready, 1)
                link(dve.tensor_scalar(score[:, 0, :], edlt[:, :], 1.0, None, ALU.add))
                link(dve.reciprocal(score[:, 0, :], score[:, 0, :]))
                link(dve.tensor_scalar(score[:, 0, :], score[:, 0, :], tanhs[:, 1:2], None, ALU.mult))
                link(dve.tensor_tensor(score[:, 1, :], score[:, 0, :], edlt[:, :], ALU.mult))

            def starts():
                dve.wait_ge(pre_done, 1)
                link(dve.tensor_copy(pre[:, :, :].rearrange("p t e -> p (t e)"), bank[5][:, 0:(NT + 1) * E]))
                link(dve.tensor_tensor(over[:, :, :], pre[:, NT, :].unsqueeze(2).to_broadcast([P, E, NT]), steps[:, :, :], ALU.is_gt))
                link(dve.tensor_reduce(nblk[:, :], over[:, :, :], AX.X, ALU.add))
                link(dve.tensor_tensor(cum[:, :, :], upto[:, :, :], nblk[:, :].unsqueeze(1).to_broadcast([P, E, E]), ALU.mult))
                link(dve.tensor_reduce(bend[:, :], cum[:, :, :], AX.X, ALU.add))
                link(dve.tensor_tensor(sstart[:, :], bend[:, :], nblk[:, :], ALU.subtract))
                link(dve.tensor_scalar(sstart[:, :], sstart[:, :], float(P), None, ALU.mult))
                link(dve.tensor_tensor(pre[:, 0:NT, :], pre[:, 0:NT, :], sstart[:, :].unsqueeze(1).to_broadcast([P, NT, E]), ALU.add))

            def slots():
                for k in range(TOPK):
                    last = dve.tensor_tensor(slotp[:, k, :, :], hot_e[:, k, :, :], pre[:, 0:NT, :], ALU.mult)
                link(last)
                link(dve.tensor_reduce(slotf[:, :], slotp[:, :, :, :].rearrange("p k t e -> p (k t) e"), AX.X, ALU.add))
                link(dve.tensor_copy(sloti[:, :], slotf[:, :]))
                dve.tensor_scalar(posi[:, 0, :], sloti[:, :], P.bit_length() - 1, None, ALU.logical_shift_right)
                link(dve.tensor_scalar(posi[:, 1, :], sloti[:, :], P - 1, None, ALU.bitwise_and))
                link(dve.tensor_copy(posf[:, :, :], posi[:, :, :]))

            def loads():
                dve.wait_ge(h_out, 48)
                link(dve.tensor_tensor(hot_b[:, :, :], iota_b[:, :].unsqueeze(1).to_broadcast([P, TOPK * NT, NB]),
                                       posf[:, 0, :].unsqueeze(2).to_broadcast([P, TOPK * NT, NB]), ALU.is_equal))
                for k in range(TOPK):
                    dve.tensor_tensor(load[:, k * NT:(k + 1) * NT, 0, :], hot_b[:, k * NT:(k + 1) * NT, :],
                                      back_of[:, :].unsqueeze(2).to_broadcast([P, NT, NB]), ALU.mult)
                dve.tensor_tensor(load[:, :, 1, :], hot_b[:, :, :],
                                  score[:, :, :].rearrange("p k t -> p (k t)").unsqueeze(2).to_broadcast([P, TOPK * NT, NB]), ALU.mult)

            def places():
                dve.tensor_tensor(hot_j, iota_j[:, :].unsqueeze(1).to_broadcast([P, TOPK * NT, P]),
                                  posf[:, 1, :].unsqueeze(2).to_broadcast([P, TOPK * NT, P]), ALU.is_equal).then_inc(load_ready, 1)

            def block_experts():
                link(dve.tensor_tensor(bge[:, :, :], iota_b[:, :].unsqueeze(2).to_broadcast([P, NB, E]),
                                       bend[:, :].unsqueeze(1).to_broadcast([P, NB, E]), ALU.is_ge))
                link(dve.tensor_reduce(bexp[:, :], bge[:, :, :], AX.X, ALU.add))
                link(dve.tensor_scalar(bexp[:, :], bexp[:, :], float(E - 1), None, ALU.min))
                link(dve.tensor_copy(bexpi[:, :], bexp[:, :]))
                link(dve.tensor_tensor(bge[:, :, :], iota_e[:, :].unsqueeze(1).to_broadcast([P, NB, E]),
                                       bexp[:, :].unsqueeze(2).to_broadcast([P, NB, E]), ALU.is_equal))

            def slot_rows():
                dve.wait_ge(tab_done, 1)
                link(dve.tensor_copy(tab[:, :, :].rearrange("p a b -> p (a b)"), bank[5][:, 0:2 * NB]))
                link(dve.tensor_scalar(padrow[:, :], tab[:, 0, :], 0.0, row_of[:, 0:1], ALU.is_equal, ALU.mult))
                link(dve.tensor_tensor(padrow[:, :], padrow[:, :], tab[:, 0, :], ALU.subtract))
                dve.tensor_scalar(rows[:, :], padrow[:, :], float(T), None, ALU.add).then_inc(rows_ready, 1)

            def factors():
                for m in range(2):
                    link(dve.tensor_tensor(bnm[:, :, :], bge[:, :, :], nexp[:, m, :].unsqueeze(1).to_broadcast([P, NB, E]), ALU.mult))
                    link(dve.tensor_reduce(bnx[:, m, :], bnm[:, :, :], AX.X, ALU.add))
                dve.tensor_scalar(silu_f[:, :].bitcast(i32), bnx[:, 0, :], 39.0, EXP, ALU.add, ALU.mult)
                dve.tensor_scalar(act_f[:, :].bitcast(i32), bnx[:, 0, :], -EXP, 181.0 * EXP, ALU.mult, ALU.add)
                link(dve.scalar_tensor_tensor(y_x[:, :], bnx[:, 0, :], 2.0, bnx[:, 1, :], ALU.mult, ALU.add))
                link(dve.tensor_scalar(y_x[:, :], y_x[:, :], -81.0, 0.0, ALU.add, ALU.max))
                link(dve.tensor_scalar(y_f[:, :].bitcast(i32), y_x[:, :], 254.0, EXP, ALU.min, ALU.mult))
                link(dve.tensor_tensor(y_f[:, :], y_f[:, :], tab[:, 1, :], ALU.mult))
                dve.tensor_scalar(y_fl[:, :], y_f[:, :], 1.0 / LOW, None, ALU.mult).then_inc(factors_ready, 1)

            def x_low(i, s):
                dve.wait_ge(xh_ready, i + 1)
                dve.scalar_tensor_tensor(xTl[s], bank[5][:, 0:D], H_SCALE, xTh[s], ALU.mult, ALU.subtract).then_inc(xl_ready, 1)

            routing = {4: [top_two], 5: [pick], 8: [starts], 9: [slots, scores], 10: [loads, places], 11: [block_experts], 13: [slot_rows], 22: [factors]}
            n_up = n_down = 0
            for s, (kind, hf, c) in enumerate(SLOTS):
                if kind == "up":
                    dve.wait_ge(ssilu_ready, n_up + 1)
                    dve.scalar_tensor_tensor(saT[:, c, :], bank[U_BANK[n_up % 2]][:, :], up_f[:, 1:2], sgs[n_up % 2],
                                             ALU.mult, ALU.mult).then_inc(sact_ready, 1)
                    n_up += 1
                else:
                    dve.wait_ge(sdown_done, n_down + 1)
                    dve.scalar_tensor_tensor(x_sb[:, n_down, :], bank[Y_BANK[n_down % 2]][:, 0:D], tanhs[:, 1:2], x_sb[:, n_down, :],
                                             ALU.mult, ALU.add).then_inc(sum_ready, 1)
                    n_down += 1
                if s == 1:
                    hT_low(1)
                if s in (20, 22):
                    x_low((s - 20) // 2, (s - 20) // 2)
                prepare(s, (2, scale1_of), (1, scale2_of), (-1, high2_of), (0, low1_of))
                for stage_ in routing.get(s, []):
                    stage_()

            def mult(i):
                dve.wait_ge(silu_ready, i + 1)
                dve.wait_ge(up_done, i + 1)
                dve.scalar_tensor_tensor(act[:, :], bank[2][:, :], act_f[:, bass.ds(i, 1)], sg, ALU.mult, ALU.mult).then_inc(act_ready, 1)

            def a_low(i):
                dve.wait_ge(ah_ready, i + 1)
                dve.scalar_tensor_tensor(aTl, aTh, -LOW, bank[6][:, :], ALU.mult, ALU.add).then_inc(al_ready, 1)

            def y_sum(i, s, added):
                dve.wait_ge(yhi_ready, i + 1)
                if added is not None:
                    dve.wait_ge(y_added, added)
                dve.scalar_tensor_tensor(ysb[s], bank[YB_BANK[s]][:, D:2 * D], y_fl[:, bass.ds(i, 1)], yhi[s],
                                         ALU.mult, ALU.add).then_inc(y_ready, 1)

            mult(0)
            for i in range(1, 4):
                x_low(i + 1, (i + 1) % 3)
                a_low(i - 1)
                mult(i)
                y_sum(i - 1, (i - 1) % 3, None)
            with dve.Fori(1, (NB - 2) // 3) as j:
                for u in range(3):
                    i = j * 3 + (u + 1)
                    x_low(i + 1, (u + 2) % 3)
                    a_low(i - 1)
                    mult(i)
                    y_sum(i - 1, u, (i - 3) * 16)
            i = NB - 1
            a_low(i - 1)
            mult(i)
            y_sum(i - 1, (i - 1) % 3, 16 * (i - 3))
            a_low(i)
            y_sum(i, i % 3, 16 * (i - 2))

        @block.scalar
        def _(se):
            def sq1_of(e):
                se.wait_ge(raw1_in[e % 2], 16 * (e // 2 + 1))
                se.activation(w1h[:, e, :, :].rearrange("p k f -> p (k f)"), stage[:, e % 2, 0:N1], ACT.Square,
                              accum_out=sumsq[:, 0, e:e + 1]).then_inc(sq1_ready, 1)

            def sq2_of(e):
                se.wait_ge(raw2_in[e % 2], 16 * (e // 2 + 1))
                se.activation(w2h[:, e, :, :].rearrange("p c d -> p (c d)"), stage[:, e % 2, N1:], ACT.Square,
                              accum_out=sumsq[:, 1, e:e + 1]).then_inc(sq2_ready, 1)

            def high1_of(e):
                se.wait_ge(scale1_ready, e + 1)
                se.activation(w1h[:, e, :, :].rearrange("p k f -> p (k f)"), stage[:, e % 2, 0:N1], ACT.Copy,
                              scale=wscale[:, 0, e:e + 1]).then_inc(high1_ready, 1)

            def shared_square(m):
                se.wait_ge((wg_in, wu_in)[m], 16)
                se.activation(wsh[:, m, :, :].rearrange("p k f -> p (k f)"), raws[:, m * NS:(m + 1) * NS], ACT.Square,
                              accum_out=sumsq_s[:, m:m + 1]).then_inc(sqs_ready, 1)

            def shared_high(m):
                se.wait_ge(scaleds_ready, m + 1)
                se.activation(wsh[:, m, :, :].rearrange("p k f -> p (k f)"), raws[:, m * NS:(m + 1) * NS], ACT.Copy).then_inc(highs_ready, 1)

            se.wait_ge(kvc_done, 1)
            se.activation(kvc_sb[:, :, :].rearrange("p t c -> p (t c)"), bank[2][:, :], ACT.Copy).then_inc(kvc_ready, 1)
            for n in range(2):
                se.wait_ge(kvT_done, n + 1)
                se.activation(kvT_sb[:, n * 512:(n + 1) * 512], bank[n][0:C, :], ACT.Copy).then_inc(kvT_ready, 1)
            for n in range(2):
                se.wait_ge(oT_done, n + 1)
                se.activation(oT_sb[:, n * 512:(n + 1) * 512], bank[3 + n][0:C, :], ACT.Copy).then_inc(oT_ready, 1)
            se.wait_ge(gate_in, 80)
            se.activation(tanhs[:, :], gates[:, :], ACT.Tanh).then_inc(tanh_ready, 1)
            shared_square(0)
            shared_square(1)
            sq1_of(0)

            def scaled(a, b):
                se.wait_ge(rs_ready, a // HT + 1)
                for t in range(a, b):
                    se.wait_ge(zc_ready, t + 1)
                    se.activation(z_sb[:, t, :], z_sb[:, t, :], ACT.Copy, scale=rs[:, t:t + 1]).then_inc(zn_ready, 1)

            def exponentials(a, b):
                for t in range(a, b):
                    se.wait_ge(max_ready, t + 1)
                    se.activation(z_sb[:, t, :], z_sb[:, t, :], ACT.Exp, bias=nmax[:, t:t + 1], scale=-1.0,
                                  accum_out=esum[:, t:t + 1]).then_inc(exp_ready, 1)

            shared_high(0)
            scaled(0, HT)
            exponentials(0, HT)
            shared_high(1)
            scaled(HT, NT)
            exponentials(HT, NT)

            def normed(hf):
                se.wait_ge(rh_ready, hf + 1)
                for t in range(hf * HT, (hf + 1) * HT):
                    se.activation(h_sb[:, t, :], x_sb[:, t, :], ACT.Identity, bias=offh[:, t:t + 1], scale=rh[:, t:t + 1]).then_inc(h_ready, 1)

            def hT_of(hf):
                for k in range(KC):
                    se.wait_ge(hT_done, hf * KC + k + 1)
                    se.activation(hTh[:, k, hf * 512:(hf + 1) * 512], bank[(5, 4)[k]][:, :], ACT.Copy, scale=H_SCALE).then_inc(hTh_ready, 1)
                for k in range(KC):
                    se.wait_ge(hTl_ready, hf * KC + k + 1)
                    se.activation(hT32[hf][:, k, :], bank[(5, 4)[k]][:, :], ACT.Copy).then_inc(hT_ready, 1)

            def x_high(i, s):
                se.wait_ge(xT_done, i + 1)
                se.activation(xTh[s], bank[5][:, 0:D], ACT.Copy, scale=H_SCALE).then_inc(xh_ready, 1)

            normed(0)
            hT_of(0)
            n_up = 0
            for s, (kind, hf, c) in enumerate(SLOTS):
                if kind == "up":
                    se.wait_ge(sup_done, n_up + 1)
                    if n_up >= 2:
                        se.wait_ge(sact_ready, n_up - 1)
                    se.activation(sgs[n_up % 2], bank[G_BANK[n_up % 2]][:, :], ACT.Silu, scale=up_f[:, 0:1]).then_inc(ssilu_ready, 1)
                    n_up += 1
                if s == 0:
                    normed(1)
                if s == 1:
                    hT_of(1)
                if s == 5:
                    se.wait_ge(dlt_ready, 1)
                    se.activation(edlt[:, :], dlt[:, :], ACT.Exp).then_inc(edlt_ready, 1)
                if s in (20, 22):
                    x_high((s - 20) // 2, (s - 20) // 2)
                prepare(s, (1, high1_of), (3, sq1_of), (2, sq2_of))

            def silu(i):
                se.wait_ge(gate_done, i + 1)
                se.activation(sg, bank[0][:, :], ACT.Silu, scale=silu_f[:, bass.ds(i, 1)]).then_inc(silu_ready, 1)

            def a_high(i):
                se.wait_ge(aT_done, i + 1)
                se.activation(aTh, bank[6][:, :], ACT.Copy, scale=1.0 / LOW).then_inc(ah_ready, 1)

            def y_high(i, s):
                se.wait_ge(y_done, i + 1)
                se.activation(yhi[s], bank[YB_BANK[s]][:, 0:D], ACT.Copy, scale=y_f[:, bass.ds(i, 1)]).then_inc(yhi_ready, 1)

            se.wait_ge(factors_ready, 1)
            silu(0)
            se.wait_ge(low1_ready, E)
            se.wait_ge(low2_ready, E)
            with se.Fori(0, (NB - 2) // 3) as j:
                for u in range(3):
                    i = j * 3 + (u + 1)
                    x_high(i + 1, (u + 2) % 3)
                    a_high(i - 1)
                    silu(i)
                    y_high(i - 1, u)
            a_high(NB - 2)
            silu(NB - 1)
            y_high(NB - 2, (NB - 2) % 3)
            a_high(NB - 1)
            y_high(NB - 1, (NB - 1) % 3)

        @block.tensor
        def _(pe):
            def warm_up(n, b):
                for _ in range(n):
                    pe.matmul(bank[b][:, :], warm[:, 0:P], warm[:, :], start=True, stop=True)

            pe.wait_ge(warm_ready, 1)
            warm_up(12, 7)
            pe.wait_ge(wk_in, 32)
            pe.wait_ge(ctxc_ready, 1)
            for t in range(NT):
                last = pe.matmul(bank[2][:, t * C:(t + 1) * C], ctxc_sb[:, t * P:(t + 1) * P], wk_sb[0:C, :], start=True, stop=True)
            last.then_inc(kvc_done, 1)
            pe.wait_ge(ctx_in, 16)
            pe.wait_ge(ones_row, 1)
            for n in range(2):
                pe.matmul(bank[n][0:C, :], wk_sb[:, :], ctx_sb[:, n * 512:(n + 1) * 512], start=True, stop=True).then_inc(kvT_done, 1)
            pe.wait_ge(kvc_ready, 1)
            pe.wait_ge(xT_in, 16)
            for b in range(NBATCH):
                o = bank[3 + b // 2][0:C, (b % 2) * TB:(b % 2 + 1) * TB]
                for k in range(KC):
                    last = pe.matmul(o, kvc_sb[:, b * KC + k, :], xT_sb[:, k, b * TB:(b + 1) * TB], start=(k == 0), stop=(k == KC - 1))
                if b % 2:
                    last.then_inc(oT_done, 1)
            pe.wait_ge(kvT_ready, 2)
            for t in range(NT):
                if t % HT == 0:
                    pe.wait_ge(oT_ready, t // HT + 1)
                b = t * P // TB
                last = pe.matmul(sim_of(t), oT_sb[:, t * P:(t + 1) * P], kvT_sb[:, b * TB:(b + 1) * TB], start=True, stop=True)
                if t % 2:
                    last.then_inc(sim_done, 1)
            pe.wait_ge(consts, 1)
            for m in range(2):
                pe.wait_ge(sqs_ready, m + 1)
                if m:
                    pe.wait_ge(scales_ready, m)
                pe.matmul(bank[6][:, 2 * E + m:2 * E + m + 1], ones[:, :], sumsq_s[:, m:m + 1], start=True, stop=True).then_inc(norms_done, 1)

            def norm1(e):
                pe.wait_ge(sq1_ready, e + 1)
                pe.wait_ge(scales_ready, 2)
                if e:
                    pe.wait_ge(scale2_ready, e)
                pe.matmul(bank[6][:, e:e + 1], ones[:, :], sumsq[:, 0, e:e + 1], start=True, stop=True).then_inc(norm1_done, 1)

            def norm2(e):
                pe.wait_ge(sq2_ready, e + 1)
                pe.wait_ge(scale1_ready, e + 1)
                pe.matmul(bank[6][:, E + e:E + e + 1], ones[:, :], sumsq[:, 1, e:e + 1], start=True, stop=True).then_inc(norm2_done, 1)

            def router(hf):
                pe.wait_ge(hT_ready, KC * (hf + 1))
                for t in range(HT):
                    tt = hf * HT + t
                    for k in range(KC):
                        last = pe.matmul(bank[3][:, tt * E:(tt + 1) * E], hT32[hf][:, k, t * P:(t + 1) * P], rw_sb[:, k, :],
                                         start=(k == 0), stop=(k == KC - 1))
                last.then_inc(logit_done, 1)

            def trans_h(hf):
                for t in range(HT):
                    if t == 0 and hf:
                        pe.wait_ge(hT_ready, KC)
                    pe.wait_ge(h_ready, hf * HT + t + 1)
                    for k in range(KC):
                        last = pe.transpose(bank[(5, 4)[k]][:, t * P:(t + 1) * P], h_sb[:, hf * HT + t, k * P:(k + 1) * P], ident[:, :])
                        if t == HT - 1:
                            last.then_inc(hT_done, 1)

            def prefix():
                pe.wait_ge(picks_ready, 1)
                NP = (NT + 1) * E
                pe.matmul(bank[5][:, 0:NP], before[:, :], picks[:, :, :].rearrange("p t e -> p (t e)"), start=True, stop=False)
                for t in range(NT):
                    last = pe.matmul(bank[5][:, (t + 1) * E:NP].rearrange("p (t e) -> p t e", e=E), ones_b[:, :],
                                     picks[:, t:t + 1, :].to_broadcast([P, NT - t, E]), start=False, stop=(t == NT - 1))
                last.then_inc(pre_done, 1)

            def table():
                pe.wait_ge(load_ready, 1)
                for n in range(TOPK * NT):
                    last = pe.matmul(bank[5][:, 0:2 * NB], hot_j[:, n, :], load[:, n, :, :].rearrange("p a b -> p (a b)"),
                                     start=(n == 0), stop=(n == TOPK * NT - 1))
                last.then_inc(tab_done, 1)

            def trans_x(i, s, count):
                pe.wait_ge(xg_in[s], count)
                if i is not None:
                    pe.wait_ge(xl_ready, i)
                for k in range(KC):
                    last = pe.transpose(bank[5][:, k * P:(k + 1) * P], xg[s][:, k * P:(k + 1) * P], ident[:, :])
                last.then_inc(xT_done, 1)

            pe.wait_ge(exp_ready, HT)
            warm_up(22, 2)
            trans_h(0)
            warm_up(10, 2)
            n_up = n_down = 0
            for s, (kind, hf, c) in enumerate(SLOTS):
                if kind == "up":
                    if n_up >= 2:
                        pe.wait_ge(sact_ready, n_up - 1)
                    if n_up == 0:
                        pe.wait_ge(lows_ready, 2)
                    if n_up in (0, SC):
                        pe.wait_ge(hTl_ready, KC * (hf + 1))
                    cols = slice(hf * 512, (hf + 1) * 512)
                    for m, b in ((0, bank[G_BANK[n_up % 2]]), (1, bank[U_BANK[n_up % 2]])):
                        for k in range(KC):
                            wh_, wl_ = (w_[:, m, k, c * P:(c + 1) * P] for w_ in (wsh, wsl))
                            pe.matmul(b[:, :], wh_, hTh[:, k, cols], start=(k == 0), stop=False)
                            pe.matmul(b[:, :], wh_, hTl[:, k, cols], start=False, stop=False)
                            last = pe.matmul(b[:, :], wl_, hTh[:, k, cols], start=False, stop=(k == KC - 1))
                    last.then_inc(sup_done, 1)
                    n_up += 1
                else:
                    if c == 0:
                        pe.wait_ge(sact_ready, SC * (hf + 1))
                        pe.wait_ge(down_in, 16)
                    if n_down >= 2:
                        pe.wait_ge(sum_ready, n_down - 1)
                    for m in range(SC):
                        last = pe.matmul(bank[Y_BANK[n_down % 2]][:, 0:D], saT[:, m, c * P:(c + 1) * P], wd_sb[:, m, :],
                                         start=(m == 0), stop=(m == SC - 1))
                    last.then_inc(sdown_done, 1)
                    n_down += 1
                if s == 0:
                    router(0)
                if s == 1:
                    trans_h(1)
                if s == 3:
                    router(1)
                if s == 7:
                    prefix()
                if s == 11:
                    table()
                prepare(s, (2, norm1), (1, norm2))
                if s == 19:
                    pe.wait_ge(rows_ready, 1)
                    trans_x(None, 0, 16)
                if s == 21:
                    trans_x(1, 1, 16)

            pe.wait_ge(low1_ready, E)
            pe.wait_ge(sact_ready, 2 * SC)

            def up_side(i, s, e, side):
                if side == 0:
                    pe.wait_ge(xl_ready, i + 1)
                for k in range(KC):
                    for x_, w_ in ((xTh, w1h), (xTh, w1l), (xTl, w1h)):
                        last = pe.matmul(bank[(0, 2)[side]][:, :], x_[s][:, k * P:(k + 1) * P],
                                         w_[:, bass.ds(e, 1), k, side * F:(side + 1) * F].rearrange("p a f -> p (a f)"),
                                         start=(k == 0 and x_ is xTh and w_ is w1h), stop=(k == KC - 1 and x_ is xTl))
                last.then_inc((gate_done, up_done)[side], 1)

            def up(i, s, e):
                up_side(i, s, e, 0)
                up_side(i, s, e, 1)

            def trans_a(i):
                pe.wait_ge(act_ready, i + 1)
                for c in range(FC):
                    last = pe.transpose(bank[6][:, c * P:(c + 1) * P], act[:, c * P:(c + 1) * P], ident[:, :])
                last.then_inc(aT_done, 1)

            def down(i, s, e, free):
                pe.wait_ge(al_ready, i + 1)
                if free is not None:
                    pe.wait_ge(y_ready, free)
                y = bank[YB_BANK[s]]
                for c in range(FC):
                    for w_ in (w2h, w2l):
                        pe.matmul(y[:, 0:D], aTh[:, c * P:(c + 1) * P], w_[:, bass.ds(e, 1), c, :].rearrange("p a d -> p (a d)"),
                                  start=(c == 0 and w_ is w2h), stop=(c == FC - 1 and w_ is w2l))
                for c in range(FC):
                    last = pe.matmul(y[:, D:2 * D], aTl[:, c * P:(c + 1) * P], w2h[:, bass.ds(e, 1), c, :].rearrange("p a d -> p (a d)"),
                                     start=(c == 0), stop=(c == FC - 1))
                last.then_inc(y_done, 1)

            def expert_of(i):
                return pe.value_load(bexpi[0:1, bass.ds(i, 1)], min_val=0, max_val=E - 1)

            up(0, 0, expert_of(0))
            pe.wait_ge(low2_ready, E)
            pe.wait_ge(sum_ready, NT)
            for i in range(1, 4):
                trans_x(i + 1, (i + 1) % 3, 16 * ((i + 1) // 3 + 1))
                trans_a(i - 1)
                up(i, i % 3, expert_of(i))
                down(i - 1, (i - 1) % 3, expert_of(i - 1), None)
            with pe.Fori(1, (NB - 2) // 3) as j:
                for u in range(3):
                    i = j * 3 + (u + 1)
                    if u == 0:
                        e_up = expert_of(i)
                    trans_x(i + 1, (u + 2) % 3, (j + (1 if u == 0 else 2)) * 16)
                    trans_a(i - 1)
                    up_side(i, (u + 1) % 3, e_up, 0)
                    if u == 0:
                        e_down = expert_of(i - 1)
                    if u < 2:
                        e_next = expert_of(i + 1)
                    up_side(i, (u + 1) % 3, e_up, 1)
                    down(i - 1, u, e_down, i - 3)
                    e_down, e_up = e_up, e_next
            i = NB - 1
            trans_a(i - 1)
            up(i, i % 3, expert_of(i))
            down(i - 1, (i - 1) % 3, expert_of(i - 1), i - 3)
            trans_a(i)
            down(i, i % 3, expert_of(i), i - 2)


_PAD = 128


def kernel(x, ctx_512, g_xattn, g_ffn, L0_xattn_W_k, L0_xattn_b_k, L0_xattn_ln_gamma, L0_xattn_ln_beta,
           L0_ffn_router_w, L0_ffn_w1, L0_ffn_w2, L0_ffn_w_gate, L0_ffn_w_up, L0_ffn_w_down):
    import numpy as np
    import concourse.bacc as bacc
    from concourse import mybir as mb
    from concourse.bass_utils import run_bass_kernel_spmd

    nc = bacc.Bacc("TRN2", target_bir_lowering=False, num_devices=1)
    B, S, D = x.shape
    x2 = np.ascontiguousarray(np.asarray(x).reshape(B * S, D))
    c2 = np.asarray(ctx_512).reshape(B * S, -1)
    ins = {
        "x": x2, "xT": x2.T, "ctxT": c2.T, "wkT": np.asarray(L0_xattn_W_k).T, "bk": L0_xattn_b_k,
        "gamma": L0_xattn_ln_gamma, "beta": L0_xattn_ln_beta, "g_att": g_xattn, "g_ffn": g_ffn,
        "rw": L0_ffn_router_w, "w1": L0_ffn_w1, "w2": L0_ffn_w2, "wg": L0_ffn_w_gate, "wu": L0_ffn_w_up, "wd": L0_ffn_w_down,
    }
    arrays, args = {}, []
    for name, a in ins.items():
        a = np.ascontiguousarray(a)
        arrays[f"in_{name}"] = a
        args.append(nc.dram_tensor(f"in_{name}", a.shape, mb.dt.from_np(a.dtype), kind="ExternalInput").ap())
    args.append(nc.dram_tensor("out_rows", (B * S + _PAD, D), mb.dt.float32, kind="ExternalOutput").ap())
    gated_attention_moe(nc, *args)
    r = run_bass_kernel_spmd(nc, [arrays], core_ids=[0])
    return r.results[0]["out_rows"][0:B * S].reshape(B, S, D)
```

```python
import concourse.bass as bass
from concourse import mybir
from contextlib import ExitStack


def gated_attention_moe(nc, x, xT, ctxT, wkT, bk, gamma, beta, g_att, g_ffn, rw, w1, w2, wg, wu, wd, out):
    f32 = mybir.dt.float32
    i32 = mybir.dt.int32
    u32 = mybir.dt.uint32
    f16 = mybir.dt.float16
    bf16 = mybir.dt.bfloat16
    ALU = mybir.AluOpType
    ACT = mybir.ActivationFunctionType
    AX = mybir.AxisListType

    P = 128
    T, D = x.shape
    NT = T // P
    HT = NT // 2
    KC = D // P
    C = ctxT.shape[0]
    NBATCH = 4
    TB = T // NBATCH
    E = rw.shape[1]
    TOPK = 2
    F2 = w1.shape[2]
    F = F2 // 2
    FC = F // P
    SI = wg.shape[1]
    SC = SI // P
    NB = (TOPK * T + E * (P - 1)) // P
    SCALE = float(D) ** -0.5
    LN_EPS, SIM_EPS = 1e-5, 1e-6
    MAGIC = float(0x5F3759DF)

    H_SCALE = 2.0 ** 11
    LOW = 2.0 ** 11
    EXP = float(2 ** 23)

    x_t = x.rearrange("(t p) d -> p t d", p=P)
    out_t = out[0:T, :].rearrange("(t p) d -> p t d", p=P)
    h_dram = nc.dram_tensor("h_rows", (T + P, D), f32).ap()
    h_t = h_dram[0:T, :].rearrange("(t p) d -> p t d", p=P)

    ctx = ExitStack()
    with ctx:
        def sb(name, shape, dt=f32):
            return ctx.enter_context(nc.sbuf_tensor(name, shape, dt))

        def sem(name):
            return ctx.enter_context(nc.semaphore(name))

        bank = [ctx.enter_context(nc.psum_tensor(f"bank{i}", [P, 512], f32)) for i in range(8)]

        x_sb = sb("x_sb", [P, NT, D])
        xT_sb = sb("xT_sb", [P, KC, T])
        h_sb = xT_sb[:, :, :].rearrange("p k (a d) -> p (k a) d", d=D)
        early = sb("early", [P, 4, T])
        ctx_sb, ctxc_sb, kvT_sb, oT_sb = early[0:C + 1, 0, :], early[0:C, 1, :], early[0:C, 2, :], early[0:C, 3, :]
        saT = early[:, :, :].rearrange("p a (b n) -> p (a b) n", n=512)
        wk_sb = sb("wk_sb", [C + 1, C])
        gambet = sb("gambet", [P, 2 * D])
        gam_sb, bet_sb = gambet[:, 0:D], gambet[:, D:2 * D]
        gates = sb("gates", [P, 2])
        tanhs = sb("tanhs", [P, 2])
        rw_sb = sb("rw_sb", [P, KC, E])
        wsh = sb("wsh", [P, 2, KC, SI], f16)
        wsl = sb("wsl", [P, 2, KC, SI], f16)
        wd_sb = sb("wd_sb", [P, SC, D])
        N1, N2 = KC * F2, FC * D
        stage = sb("stage", [P, 2, N1 + N2])
        w1h = sb("w1h", [P, E, KC, F2], f16)
        w1l = sb("w1l", [P, E, KC, F2], f16)
        w2h = sb("w2h", [P, E, FC, D], f16)
        w2l = sb("w2l", [P, E, FC, D], f16)
        NS = KC * SI
        raws = w1l[:, E // 2:, :, :].rearrange("p e k f -> p (e k f)").bitcast(f32)
        warm = sb("warm", [P, 2 * D], bf16)
        zeros = warm[:, :].bitcast(f32)
        ident = sb("ident", [P, P])
        before = sb("before", [P, P], bf16)
        ones = sb("ones", [P, P])
        ones_b = sb("ones_b", [P, P], bf16)
        iota_e = sb("iota_e", [P, E])
        iota_b = sb("iota_b", [P, NB])
        iota_j = sb("iota_j", [P, P])
        row_of = sb("row_of", [P, 1])
        back_of = sb("back_of", [P, NT], f16)
        steps = sb("steps", [P, E, NT])
        upto = sb("upto", [P, E, E])
        cmean = sb("cmean", [C, NBATCH])
        kvc_sb = sb("kvc_sb", [P, NT, C])
        stats = sb("stats", [P, NT, 6])
        mvx = sb("mvx", [P, NT, 2])
        mvs = sb("mvs", [P, NT, 2])
        mvh = sb("mvh", [P, NT, 2])
        var = sb("var", [P, NT])
        r_y = sb("r_y", [P, NT])
        r_p = sb("r_p", [P, NT])
        r_q = sb("r_q", [P, NT])
        rx = sb("rx", [P, NT])
        rs = sb("rs", [P, NT])
        rh = sb("rh", [P, NT])
        offh = sb("offh", [P, NT])
        nmax = sb("nmax", [P, NT])
        esum = sb("esum", [P, NT])
        einv = sb("einv", [P, NT])
        mid = sb("mid", [P, NT, D])
        z_sb = mid[:, :, :]
        hT32 = [mid[:, i * HT:(i + 1) * HT, :].rearrange("p t d -> p (t d)").rearrange("p (k n) -> p k n", k=KC) for i in range(2)]
        hot_j = mid[:, 0:HT, :].rearrange("p t d -> p (t d)").bitcast(f16).rearrange("p (n j) -> p n j", j=P)
        hTh = sb("hTh", [P, KC, T], f16)
        hTl = sb("hTl", [P, KC, T], f16)
        spare = xT_sb[:, :, :].rearrange("p k t -> p (k t)")
        load = spare[:, 0:TOPK * NT * 2 * NB].bitcast(f16).rearrange("p (n a b) -> p n a b", a=4, b=NB)
        spare = spare[:, TOPK * NT * 2 * NB:]
        hot_b = spare[:, 0:TOPK * NT * NB].bitcast(f16)[:, 0:TOPK * NT * NB].rearrange("p (n b) -> p n b", b=NB)
        spare = spare[:, TOPK * NT * NB:]
        bge = spare[:, 0:NB * E].rearrange("p (b e) -> p b e", e=E)
        bnm = spare[:, NB * E:2 * NB * E].rearrange("p (b e) -> p b e", e=E)
        act = spare[:, 2 * NB * E:2 * NB * E + F]
        logit = sb("logit", [P, NT, E])
        top = sb("top", [P, NT, 8])
        topi = sb("topi", [P, NT, 8], u32)
        idxf = sb("idxf", [P, TOPK, NT])
        hot_e = sb("hot_e", [P, TOPK, NT, E])
        picks = sb("picks", [P, NT + 1, E], bf16)
        dlt = sb("dlt", [P, NT])
        edlt = sb("edlt", [P, NT])
        score = sb("score", [P, TOPK, NT])
        rest = sb("rest", [P, 2, TOPK * NT])
        parts = sb("parts", [P, 3, TOPK * NT], f16)
        pre = sb("pre", [P, NT + 1, E])
        over = sb("over", [P, E, NT])
        nblk = sb("nblk", [P, E])
        cum = sb("cum", [P, E, E])
        bend = sb("bend", [P, E])
        sstart = sb("sstart", [P, E])
        slotp = mid[:, NT - 1, 0:TOPK * NT * E].rearrange("p (k t e) -> p k t e", k=TOPK, e=E)
        slotf = sb("slotf", [P, TOPK * NT])
        sloti = sb("sloti", [P, TOPK * NT], i32)
        posi = sb("posi", [P, 2, TOPK * NT], i32)
        posf = sb("posf", [P, 2, TOPK * NT])
        tab = sb("tab", [P, 4, NB])
        padrow = sb("padrow", [P, NB])
        rows = sb("rows", [P, NB], i32)
        bexp = sb("bexp", [P, NB])
        bexpi = sb("bexpi", [P, NB], i32)
        sumsq_s = sb("sumsq_s", [P, 2])
        nexp_s = sb("nexp_s", [P, 2], i32)
        wscale_s = sb("wscale_s", [P, 2])
        up_f = sb("up_f", [P, 2])
        sumsq = sb("sumsq", [P, 2, E])
        nexp_i = sb("nexp_i", [P, 2, E], i32)
        nexp = sb("nexp", [P, 2, E])
        wscale = sb("wscale", [P, 2, E])
        bnx = sb("bnx", [P, 2, NB])
        silu_f = sb("silu_f", [P, NB])
        act_f = sb("act_f", [P, NB])
        y_x = sb("y_x", [P, NB])
        y_f = sb("y_f", [P, NB])
        y_fl = sb("y_fl", [P, NB])
        sg = sb("sg", [P, 512])[:, :]
        sgs = (sg, gambet[:, :], mid[:, HT + 2:, :].rearrange("p t d -> p (t d)"))
        flat = mid[:, :, :].rearrange("p t d -> p (t d)")
        xg = [flat[:, i * D:(i + 1) * D] for i in range(3)]
        half = flat[:, 3 * D:6 * D].bitcast(f16)
        xTh = [half[:, (2 * i) * D:(2 * i + 1) * D] for i in range(3)]
        xTl = [half[:, (2 * i + 1) * D:(2 * i + 2) * D] for i in range(3)]
        flat = stage[:, :, :].rearrange("p a n -> p (a n)")
        ysb = [flat[:, i * D:(i + 1) * D] for i in range(3)]
        yhi = [flat[:, (3 + i) * D:(4 + i) * D] for i in range(3)]
        half = flat[:, 6 * D:8 * D].bitcast(f16)
        aTh, aTl = half[:, 0:2 * D], half[:, 2 * D:4 * D]

        ctx_in, wk_in, gate_in, wg_in, wu_in, down_in = (
            sem(n) for n in ("ctx_in", "wk_in", "gate_in", "wg_in", "wu_in", "down_in"))
        x_in = [sem(f"x_in{i}") for i in range(2)]
        xT_in = [sem(f"xT_in{i}") for i in range(2)]
        raw1_in = [sem(f"raw1_in{i}") for i in range(2)]
        raw2_in = [sem(f"raw2_in{i}") for i in range(2)]
        consts, pool_step, ones_row, warm_ready = sem("consts"), sem("pool_step"), sem("ones_row"), sem("warm_ready")
        dve_step = sem("dve_step")
        ctxc_ready, kvT_done, kvc_done, kvT_ready, kvc_ready = (sem(n) for n in ("ctxc_ready", "kvT_done", "kvc_done", "kvT_ready", "kvc_ready"))
        oT_done, oT_ready, sim_done, rs_ready, zc_ready, zn_ready = (sem(n) for n in ("oT_done", "oT_ready", "sim_done", "rs_ready", "zc_ready", "zn_ready"))
        x1_ready = sem("x1_ready")
        tanh_ready, max_ready, exp_ready, rh_ready, h_ready, h_out = (sem(n) for n in ("tanh_ready", "max_ready", "exp_ready", "rh_ready", "h_ready", "h_out"))
        hT_done, hT_ready, logit_done, dlt_ready, edlt_ready = (sem(n) for n in ("hT_done", "hT_ready", "logit_done", "dlt_ready", "edlt_ready"))
        picks_ready, pre_done, load_ready, tab_done, rows_ready, factors_ready = (sem(n) for n in ("picks_ready", "pre_done", "load_ready", "tab_done", "rows_ready", "factors_ready"))
        sup_done, ssilu_ready, sact_ready, sdown_done, sum_ready, sum_out = (sem(n) for n in ("sup_done", "ssilu_ready", "sact_ready", "sdown_done", "sum_ready", "sum_out"))
        sq1_ready, norm1_done, scale1_ready, high1_ready, low1_ready = (sem(n) for n in ("sq1_ready", "norm1_done", "scale1_ready", "high1_ready", "low1_ready"))
        sq2_ready, norm2_done, scale2_ready, high2_ready, low2_ready = (sem(n) for n in ("sq2_ready", "norm2_done", "scale2_ready", "high2_ready", "low2_ready"))
        scaled2_ready = sem("scaled2_ready")
        parts_ready = sem("parts_ready")
        sqs_ready, norms_done, scales_ready, scaleds_ready, highs_ready, lows_ready = (
            sem(n) for n in ("sqs_ready", "norms_done", "scales_ready", "scaleds_ready", "highs_ready", "lows_ready"))
        hTh_ready, hTl_ready = sem("hTh_ready"), sem("hTl_ready")
        xg_in = [sem(f"xg_in{i}") for i in range(3)]
        xT_done, xh_ready, xl_ready, gate_done, up_done, silu_ready, act_ready = (
            sem(n) for n in ("xgT_done", "xh_ready", "xl_ready", "gate_done", "up_done", "silu_ready", "act_ready"))
        aT_done, ah_ready, al_ready, y_done, yhi_ready, y_ready, y_added = (
            sem(n) for n in ("aT_done", "ah_ready", "al_ready", "y_done", "yhi_ready", "y_ready", "y_added"))

        SIM_BANK = (0, 1, 5, 7)
        G_BANK, U_BANK, Y_BANK = (0, 1, 3), (2, 7, 4), (3, 4, 7)

        def turn(hf, c):
            return c % (2 + hf)

        def sim_of(t):
            return bank[SIM_BANK[t // 2]][:, (t % 2) * D:(t % 2 + 1) * D]

        SLOTS = []
        for hf in range(2):
            SLOTS += [("up", hf, c) for c in range(SC)] + [("down", hf, t) for t in range(HT)]

        BASE = (2, 5, 8, 11, 14, 16, 20, 22)
        ROUTER_SLOTS = (0, 3)
        SECOND_HALF_SLOT = 2
        PREFIX_SLOT = 8
        SCORE_SLOT = 8
        TABLE_SLOT = 14
        BLOCK_SLOTS = (20, 22)
        GATHER_AFTER = 5

        def prepare(k, *what):
            for lead, step in what:
                for e in range(E):
                    if BASE[e] - lead == k:
                        step(e)

        block = ctx.enter_context(nc.Block())

        @block.sync
        def _(sp):
            def raw1(e):
                for k in range(KC):
                    if e >= 2:
                        sp.wait_ge(low1_ready, KC * (e - 2) + k + 1)
                    sp.dma_start(stage[:, e % 2, k * F2:(k + 1) * F2], w1[e, k * P:(k + 1) * P, :]).then_inc(raw1_in[e % 2], 16)

            def raw2(e):
                sp.dma_start(stage[:, e % 2, N1:].rearrange("p (c d) -> p c d", c=FC),
                             w2[e].rearrange("(c p) d -> p c d", p=P)).then_inc(raw2_in[e % 2], 16)

            sp.dma_start(ctx_sb[0:C, :], ctxT).then_inc(ctx_in, 16)
            sp.dma_start(wk_sb[0:C, :], wkT).then_inc(wk_in, 16)
            sp.dma_start(wk_sb[C:C + 1, :], bk.rearrange("(a n) -> a n", a=1)).then_inc(wk_in, 16)
            for hf in range(2):
                sp.dma_start(xT_sb[:, :, hf * 512:(hf + 1) * 512], xT[:, hf * 512:(hf + 1) * 512].rearrange("(k p) t -> p k t", p=P)).then_inc(xT_in[hf], 16)
                sp.dma_start(x_sb[:, hf * HT:(hf + 1) * HT, :], x_t[:, hf * HT:(hf + 1) * HT, :]).then_inc(x_in[hf], 16)
            sp.dma_start(gates[:, 0:1], g_att.partition_broadcast(P)).then_inc(gate_in, 16)
            sp.dma_start(gates[:, 1:2], g_ffn.partition_broadcast(P)).then_inc(gate_in, 16)
            sp.dma_start(gam_sb, gamma.partition_broadcast(P)).then_inc(gate_in, 16)
            sp.dma_start(bet_sb, beta.partition_broadcast(P)).then_inc(gate_in, 16)
            sp.dma_start(rw_sb[:, :, :], rw.rearrange("(k p) e -> p k e", p=P)).then_inc(gate_in, 16)
            sp.dma_start(raws[:, 0:NS].rearrange("p (k f) -> p k f", k=KC), wg.rearrange("(k p) f -> p k f", p=P)).then_inc(wg_in, 16)
            sp.dma_start(raws[:, NS:].rearrange("p (k f) -> p k f", k=KC), wu.rearrange("(k p) f -> p k f", p=P)).then_inc(wu_in, 16)
            raw1(0)
            raw2(0)
            raw1(1)
            raw2(1)
            sp.dma_start(wd_sb[:, :, :], wd.rearrange("(c p) d -> p c d", p=P)).then_inc(down_in, 16)
            sp.wait_ge(warm_ready, 1)
            sp.dma_start(h_dram[T:T + P, :], zeros).then_inc(h_out, 16)
            sp.dma_start(out[T:T + P, :], zeros).then_inc(sum_out, 16)
            for hf in range(2):
                sp.wait_ge(h_ready, HT * (hf + 1))
                sp.dma_start(h_t[:, hf * HT:(hf + 1) * HT, :], h_sb[:, hf * HT:(hf + 1) * HT, :]).then_inc(h_out, 16)
            for e in range(2, E):
                raw1(e)
                sp.wait_ge(low2_ready, e - 1)
                raw2(e)
            for hf in range(2):
                sp.wait_ge(sum_ready, HT * (hf + 1))
                sp.dma_start(out_t[:, hf * HT:(hf + 1) * HT, :], x_sb[:, hf * HT:(hf + 1) * HT, :]).then_inc(sum_out, 16)
            sp.wait_ge(h_out, 48)
            sp.wait_ge(sum_out, 48)
            sp.wait_ge(y_added, 16 * NB)

        @block.gpsimd
        def _(pool):
            pool.memset(ctx_sb[C:C + 1, :], 1.0).then_inc(ones_row, 1)
            pool.wait_ge(ones_row, 1)
            pool.memset(ident[:, :], 0.0)
            pool.memset(before[:, :], 1.0)
            pool.memset(upto[:, :, :], 1.0)
            pool.memset(ones[:, :], 1.0)
            pool.memset(ones_b[:, :], 1.0)
            pool.iota(iota_e[:, :], [[1, E]], base=0, channel_multiplier=0, allow_small_or_imprecise_dtypes=True)
            pool.iota(iota_b[:, :], [[1, NB]], base=0, channel_multiplier=0, allow_small_or_imprecise_dtypes=True)
            pool.iota(iota_j[:, :], [[1, P]], base=0, channel_multiplier=0, allow_small_or_imprecise_dtypes=True)
            pool.iota(row_of[:, :], [[1, 1]], base=0, channel_multiplier=1, allow_small_or_imprecise_dtypes=True)
            pool.iota(back_of[:, :], [[-P, NT]], base=T, channel_multiplier=-1, allow_small_or_imprecise_dtypes=True)
            pool.iota(steps[:, :, :], [[0, E], [P, NT]], base=0, channel_multiplier=0,
                      allow_small_or_imprecise_dtypes=True).then_inc(pool_step, 1)
            pool.wait_ge(pool_step, 1)
            pool.affine_select(out=ident[:, :], in_=ident[:, :], compare_op=ALU.not_equal, fill=1.0,
                               base=0, pattern=[[-1, P]], channel_multiplier=1)
            pool.affine_select(out=before[:, :], in_=before[:, :], compare_op=ALU.is_gt, fill=0.0,
                               base=0, pattern=[[1, P]], channel_multiplier=-1)
            pool.affine_select(out=upto[:, :, :], in_=upto[:, :, :], compare_op=ALU.is_ge, fill=0.0,
                               base=0, pattern=[[1, E], [-1, E]], channel_multiplier=0).then_inc(consts, 1)
            def wide(scale, n):
                return scale.to_broadcast([P, n])

            for m in range(2):
                pool.wait_ge(scales_ready, m + 1)
                pool.tensor_tensor(raws[:, m * NS:(m + 1) * NS], raws[:, m * NS:(m + 1) * NS], wide(wscale_s[:, m:m + 1], NS),
                                   ALU.mult).then_inc(scaleds_ready, 1)
            for m in range(2):
                pool.wait_ge(highs_ready, m + 1)
                pool.tensor_tensor(wsl[:, m, :, :].rearrange("p k f -> p (k f)"), raws[:, m * NS:(m + 1) * NS],
                                   wsh[:, m, :, :].rearrange("p k f -> p (k f)"), ALU.subtract).then_inc(lows_ready, 1)

            def gather(b):
                pool.indirect_dma_start(out=xg[b % 3], out_offset=None, in_=h_dram,
                                        in_offset=bass.IndirectOffsetOnAxis(ap=rows[:, b:b + 1], axis=0)
                                        ).then_inc(xg_in[b % 3], 16)

            for e in range(E):
                pool.wait_ge(scale2_ready, e + 1)
                pool.tensor_tensor(stage[:, e % 2, N1:], stage[:, e % 2, N1:], wide(wscale[:, 1, e:e + 1], N2), ALU.mult).then_inc(scaled2_ready, 1)
                pool.wait_ge(high2_ready, e + 1)
                pool.tensor_tensor(w2l[:, e, :, :].rearrange("p c d -> p (c d)"), stage[:, e % 2, N1:],
                                   w2h[:, e, :, :].rearrange("p c d -> p (c d)"), ALU.subtract).then_inc(low2_ready, 1)
                if e == GATHER_AFTER:
                    pool.wait_ge(h_out, 48)
                    pool.wait_ge(rows_ready, 1)
                    for b in range(3):
                        gather(b)
            pool.wait_ge(xT_done, 1)
            gather(3)
            pool.wait_ge(sum_out, 48)
            for b in range(NB):
                if b + 4 < NB:
                    pool.wait_ge(xT_done, b + 2)
                    gather(b + 4)
                pool.wait_ge(y_ready, b + 1)
                if b:
                    pool.wait_ge(y_added, 16 * b)
                pool.indirect_dma_start(out=out, out_offset=bass.IndirectOffsetOnAxis(ap=rows[:, b:b + 1], axis=0),
                                        in_=ysb[b % 3], in_offset=None, compute_op=ALU.add).then_inc(y_added, 16)

        @block.vector
        def _(dve):
            steps_done = [0]

            def link(ins, between=()):
                steps_done[0] += 1
                ins.then_inc(dve_step, 1)
                if between:
                    between.pop(0)()
                dve.wait_ge(dve_step, steps_done[0])

            def mark(ins):
                steps_done[0] += 1
                ins.then_inc(dve_step, 1)

            def rsqrt(to, v, a, b, between=()):
                y, p, q = r_y[:, a:b], r_p[:, a:b], r_q[:, a:b]
                link(dve.tensor_scalar(y.bitcast(i32), v.bitcast(i32), 1, None, ALU.logical_shift_right), between)
                link(dve.tensor_scalar(y.bitcast(i32), y.bitcast(i32), -1.0, MAGIC, ALU.mult, ALU.add), between)
                for n in range(3):
                    link(dve.tensor_tensor(p, y, y, ALU.mult), between)
                    link(dve.scalar_tensor_tensor(q, p, -0.5, v, ALU.mult, ALU.mult), between)
                    link(dve.scalar_tensor_tensor(to if n == 2 else y, q, 1.5, y, ALU.add, ALU.mult), between)

            def scale_of(e, m, norm_done, scale_ready):
                dve.wait_ge(norm_done, e + 1)
                link(dve.tensor_scalar(nexp_i[:, m, e:e + 1], bank[6][:, m * E + e:m * E + e + 1].bitcast(i32), 24, None, ALU.logical_shift_right))
                dve.tensor_copy(nexp[:, m, e:e + 1], nexp_i[:, m, e:e + 1])
                dve.tensor_scalar(wscale[:, m, e:e + 1].bitcast(i32), nexp_i[:, m, e:e + 1], -EXP, 204.0 * EXP,
                                  ALU.mult, ALU.add).then_inc(scale_ready, 1)

            def scale1_of(e):
                scale_of(e, 0, norm1_done, scale1_ready)

            def scale2_of(e):
                scale_of(e, 1, norm2_done, scale2_ready)

            def low1_of(e):
                dve.wait_ge(high1_ready, e + 1)
                for k in range(KC):
                    dve.scalar_tensor_tensor(w1l[:, e, k, :], stage[:, e % 2, k * F2:(k + 1) * F2], wscale[:, 0, e:e + 1],
                                             w1h[:, e, k, :], ALU.mult, ALU.subtract).then_inc(low1_ready, 1)

            def high2_of(e):
                dve.wait_ge(scaled2_ready, e + 1)
                dve.tensor_copy(w2h[:, e, :, :].rearrange("p c d -> p (c d)"), stage[:, e % 2, N1:]).then_inc(high2_ready, 1)

            def shared_exponent(m):
                def run():
                    dve.wait_ge(norms_done, m + 1)
                    mark(dve.tensor_scalar(nexp_s[:, m:m + 1], bank[6][:, 2 * E + m:2 * E + m + 1].bitcast(i32), 24, None, ALU.logical_shift_right))
                return run

            def shared_scale(m):
                def run():
                    dve.tensor_scalar(wscale_s[:, m:m + 1].bitcast(i32), nexp_s[:, m:m + 1], -EXP, 204.0 * EXP, ALU.mult, ALU.add).then_inc(scales_ready, 1)
                    dve.tensor_scalar(up_f[:, m:m + 1].bitcast(i32), nexp_s[:, m:m + 1], 39.0, EXP, ALU.add, ALU.mult)
                return run

            dve.memset(warm[:, :], 0.0).then_inc(warm_ready, 1)
            dve.wait_ge(ctx_in, 16)
            link(dve.tensor_reduce(cmean[:, :], ctx_sb[0:C, :].rearrange("c (b j) -> c b j", b=NBATCH), AX.X, ALU.add))
            link(dve.tensor_scalar(cmean[:, :], cmean[:, :], -1.0 / TB, None, ALU.mult))
            for b in range(NBATCH):
                last = dve.tensor_scalar(ctxc_sb[:, b * TB:(b + 1) * TB], ctx_sb[0:C, b * TB:(b + 1) * TB],
                                         cmean[:, b:b + 1], None, ALU.add)
            last.then_inc(ctxc_ready, 1)
            for t in range(NT):
                if t % HT == 0:
                    dve.wait_ge(x_in[t // HT], 16)
                last = dve.bn_stats(stats[:, t, :], x_sb[:, t, :])
            link(last)
            for t in range(NT):
                last = dve.bn_aggr(mvx[:, t, :], stats[:, t, :])
            link(last)
            link(dve.tensor_scalar(var[:, :], mvx[:, :, 1], LN_EPS, None, ALU.add))
            rsqrt(rx[:, :], var[:, :], 0, NT)
            link(dve.tensor_scalar(rx[:, :], rx[:, :], SCALE, None, ALU.mult))

            def sim_stats(t):
                if t % 2 == 0:
                    dve.wait_ge(sim_done, t // 2 + 1)
                mark(dve.bn_stats(stats[:, t, :], sim_of(t)))

            def centred(t):
                return lambda: dve.scalar_tensor_tensor(z_sb[:, t, :], sim_of(t), mvs[:, t, 0:1], gam_sb,
                                                        ALU.subtract, ALU.mult).then_inc(zc_ready, 1)

            def sim_variance(a, b, between):
                for t in range(a, b):
                    last = dve.bn_aggr(mvs[:, t, :], stats[:, t, :])
                link(last)
                link(dve.tensor_tensor(var[:, a:b], rx[:, a:b], rx[:, a:b], ALU.mult), between)
                link(dve.tensor_tensor(var[:, a:b], var[:, a:b], mvs[:, a:b, 1], ALU.mult), between)
                link(dve.tensor_scalar(var[:, a:b], var[:, a:b], SIM_EPS, None, ALU.add), between)

            def sim_factor(a, b, root):
                dve.scalar_tensor_tensor(rs[:, a:b], root, -1.0, rx[:, a:b], ALU.mult, ALU.mult).then_inc(rs_ready, 1)

            def largest(t):
                def run():
                    dve.wait_ge(zn_ready, t + 1)
                    dve.tensor_tensor_reduce(out=z_sb[:, t, :], in0=z_sb[:, t, :], in1=bet_sb, scale=1.0, scalar=3.0e38,
                                             op0=ALU.add, op1=ALU.min, accum_out=nmax[:, t:t + 1]).then_inc(max_ready, 1)
                return run

            def weights(a, b, between=()):
                dve.wait_ge(exp_ready, b)
                link(dve.reciprocal(einv[:, a:b], esum[:, a:b]), between)
                link(dve.tensor_scalar(einv[:, a:b], einv[:, a:b], tanhs[:, 0:1], None, ALU.mult), between)

            def attended(t):
                return lambda: dve.scalar_tensor_tensor(x_sb[:, t, :], z_sb[:, t, :], einv[:, t:t + 1], x_sb[:, t, :],
                                                        ALU.mult, ALU.add).then_inc(x1_ready, 1)

            def stats_of(t):
                dve.wait_ge(x1_ready, t + 1)
                mark(dve.bn_stats(stats[:, t, :], x_sb[:, t, :]))

            def norm_variance(a, b):
                for t in range(a, b):
                    last = dve.bn_aggr(mvh[:, t, :], stats[:, t, :])
                link(last)
                link(dve.tensor_scalar(var[:, a:b], mvh[:, a:b, 1], LN_EPS, None, ALU.add))

            def norm_offset(a, b):
                dve.scalar_tensor_tensor(offh[:, a:b], rh[:, a:b], -1.0, mvh[:, a:b, 0], ALU.mult, ALU.mult).then_inc(rh_ready, 1)

            def settle():
                dve.wait_ge(dve_step, steps_done[0])

            dve.wait_ge(gate_in, 80)
            link(dve.tensor_scalar(bet_sb, bet_sb, -1.0, None, ALU.mult))
            for t in range(HT):
                sim_stats(t)
            settle()
            between = [centred(t) for t in range(HT)] + [shared_exponent(0), shared_scale(0)]
            sim_variance(0, HT, between)
            rsqrt(rs[:, 0:HT], var[:, 0:HT], 0, HT, between)
            assert not between
            sim_factor(0, HT, rs[:, 0:HT])
            for t in range(HT, NT):
                sim_stats(t)
            settle()
            between = [shared_exponent(1), shared_scale(1), largest(0)]
            sim_variance(HT, NT, between)
            assert not between
            for t in range(1, HT):
                largest(t)()
            for t in range(HT, NT - 1):
                centred(t)()
            weights(0, HT)
            for t in range(HT):
                attended(t)()
            for t in range(HT):
                stats_of(t)
            settle()
            norm_variance(0, HT)
            between = [centred(NT - 1)]
            rsqrt(rh[:, :], var[:, :], 0, NT, between)
            assert not between
            norm_offset(0, HT)
            sim_factor(HT, NT, rh[:, HT:NT])

            def hT_low(hf):
                for k in range(KC):
                    dve.wait_ge(hTh_ready, hf * KC + k + 1)
                    dve.scalar_tensor_tensor(hTl[:, k, hf * 512:(hf + 1) * 512], bank[(5, 4)[k]][:, :], H_SCALE,
                                             hTh[:, k, hf * 512:(hf + 1) * 512], ALU.mult, ALU.subtract).then_inc(hTl_ready, 1)

            def normed(hf):
                dve.wait_ge(rh_ready, hf + 1)
                for t in range(hf * HT, (hf + 1) * HT):
                    dve.tensor_scalar(h_sb[:, t, :], x_sb[:, t, :], rh[:, t:t + 1], offh[:, t:t + 1], ALU.mult, ALU.add).then_inc(h_ready, 1)

            normed(0)
            for t in range(HT, NT):
                largest(t)()
            hT_low(0)
            weights(HT, NT)
            for t in range(HT, NT):
                attended(t)()

            for t in range(HT, NT):
                stats_of(t)
            settle()

            def top_two():
                dve.wait_ge(logit_done, 2)
                link(dve.tensor_copy(logit[:, :, :].rearrange("p t e -> p (t e)"), bank[3][:, 0:NT * E]))
                for t in range(NT):
                    last = dve.max(top[:, t, :], logit[:, t, :])
                link(last)
                dve.tensor_tensor(dlt[:, :], top[:, :, 1], top[:, :, 0], ALU.subtract).then_inc(dlt_ready, 1)

            def pick():
                for t in range(NT):
                    last = dve.max_index(topi[:, t, :], top[:, t, :], logit[:, t, :])
                link(last)
                link(dve.tensor_copy(idxf[:, :, :], topi[:, :, 0:TOPK].rearrange("p t k -> p k t")))
                link(dve.tensor_tensor(hot_e[:, :, :, :].rearrange("p k t e -> p (k t) e"),
                                       iota_e[:, :].unsqueeze(1).to_broadcast([P, TOPK * NT, E]),
                                       idxf[:, :, :].rearrange("p k t -> p (k t)").unsqueeze(2).to_broadcast([P, TOPK * NT, E]),
                                       ALU.is_equal))
                dve.memset(picks[:, NT, :], 0.0)
                dve.tensor_tensor(picks[:, 0:NT, :], hot_e[:, 0, :, :], hot_e[:, 1, :, :], ALU.add).then_inc(picks_ready, 1)

            def scores():
                dve.wait_ge(edlt_ready, 1)
                link(dve.tensor_scalar(score[:, 0, :], edlt[:, :], 1.0, None, ALU.add))
                link(dve.reciprocal(score[:, 0, :], score[:, 0, :]))
                link(dve.tensor_scalar(score[:, 0, :], score[:, 0, :], tanhs[:, 1:2], None, ALU.mult))
                link(dve.tensor_tensor(score[:, 1, :], score[:, 0, :], edlt[:, :], ALU.mult))

            def score_parts():
                whole = score[:, :, :].rearrange("p k t -> p (k t)")
                link(dve.tensor_copy(parts[:, 0, :], whole))
                link(dve.tensor_tensor(rest[:, 0, :], whole, parts[:, 0, :], ALU.subtract))
                link(dve.tensor_scalar(parts[:, 1, :], rest[:, 0, :], LOW, None, ALU.mult))
                link(dve.scalar_tensor_tensor(rest[:, 1, :], rest[:, 0, :], LOW, parts[:, 1, :], ALU.mult, ALU.subtract))
                link(dve.tensor_scalar(parts[:, 2, :], rest[:, 1, :], LOW, None, ALU.mult))

            def starts():
                dve.wait_ge(pre_done, 1)
                link(dve.tensor_copy(pre[:, :, :].rearrange("p t e -> p (t e)"), bank[5][:, 0:(NT + 1) * E]))
                link(dve.tensor_tensor(over[:, :, :], pre[:, NT, :].unsqueeze(2).to_broadcast([P, E, NT]), steps[:, :, :], ALU.is_gt))
                link(dve.tensor_reduce(nblk[:, :], over[:, :, :], AX.X, ALU.add))
                link(dve.tensor_tensor(cum[:, :, :], upto[:, :, :], nblk[:, :].unsqueeze(1).to_broadcast([P, E, E]), ALU.mult))
                link(dve.tensor_reduce(bend[:, :], cum[:, :, :], AX.X, ALU.add))
                link(dve.tensor_tensor(sstart[:, :], bend[:, :], nblk[:, :], ALU.subtract))
                link(dve.tensor_scalar(sstart[:, :], sstart[:, :], float(P), None, ALU.mult))
                link(dve.tensor_tensor(pre[:, 0:NT, :], pre[:, 0:NT, :], sstart[:, :].unsqueeze(1).to_broadcast([P, NT, E]), ALU.add))

            def slots():
                for k in range(TOPK):
                    last = dve.tensor_tensor(slotp[:, k, :, :], hot_e[:, k, :, :], pre[:, 0:NT, :], ALU.mult)
                link(last)
                link(dve.tensor_reduce(slotf[:, :], slotp[:, :, :, :].rearrange("p k t e -> p (k t) e"), AX.X, ALU.add))
                link(dve.tensor_copy(sloti[:, :], slotf[:, :]))
                dve.tensor_scalar(posi[:, 0, :], sloti[:, :], P.bit_length() - 1, None, ALU.logical_shift_right)
                link(dve.tensor_scalar(posi[:, 1, :], sloti[:, :], P - 1, None, ALU.bitwise_and))
                link(dve.tensor_copy(posf[:, :, :], posi[:, :, :]))

            def loads():
                dve.wait_ge(h_out, 48)
                link(dve.tensor_tensor(hot_b[:, :, :], iota_b[:, :].unsqueeze(1).to_broadcast([P, TOPK * NT, NB]),
                                       posf[:, 0, :].unsqueeze(2).to_broadcast([P, TOPK * NT, NB]), ALU.is_equal))
                for k in range(TOPK):
                    dve.tensor_tensor(load[:, k * NT:(k + 1) * NT, 0, :], hot_b[:, k * NT:(k + 1) * NT, :],
                                      back_of[:, :].unsqueeze(2).to_broadcast([P, NT, NB]), ALU.mult)

            def load_parts():
                for m in range(3):
                    last = dve.tensor_tensor(load[:, :, m + 1, :], hot_b[:, :, :],
                                             parts[:, m, :].unsqueeze(2).to_broadcast([P, TOPK * NT, NB]), ALU.mult)
                last.then_inc(parts_ready, 1)

            def places():
                dve.tensor_tensor(hot_j, iota_j[:, :].unsqueeze(1).to_broadcast([P, TOPK * NT, P]),
                                  posf[:, 1, :].unsqueeze(2).to_broadcast([P, TOPK * NT, P]), ALU.is_equal).then_inc(load_ready, 1)

            def block_experts():
                link(dve.tensor_tensor(bge[:, :, :], iota_b[:, :].unsqueeze(2).to_broadcast([P, NB, E]),
                                       bend[:, :].unsqueeze(1).to_broadcast([P, NB, E]), ALU.is_ge))
                link(dve.tensor_reduce(bexp[:, :], bge[:, :, :], AX.X, ALU.add))
                link(dve.tensor_scalar(bexp[:, :], bexp[:, :], float(E - 1), None, ALU.min))
                link(dve.tensor_copy(bexpi[:, :], bexp[:, :]))
                link(dve.tensor_tensor(bge[:, :, :], iota_e[:, :].unsqueeze(1).to_broadcast([P, NB, E]),
                                       bexp[:, :].unsqueeze(2).to_broadcast([P, NB, E]), ALU.is_equal))

            def slot_rows():
                dve.wait_ge(tab_done, 1)
                link(dve.tensor_copy(tab[:, :, :].rearrange("p a b -> p (a b)"), bank[5][:, 0:4 * NB]))
                link(dve.scalar_tensor_tensor(tab[:, 2, :], tab[:, 3, :], 1.0 / LOW, tab[:, 2, :], ALU.mult, ALU.add))
                link(dve.scalar_tensor_tensor(tab[:, 1, :], tab[:, 2, :], 1.0 / LOW, tab[:, 1, :], ALU.mult, ALU.add))
                link(dve.tensor_scalar(padrow[:, :], tab[:, 0, :], 0.0, row_of[:, 0:1], ALU.is_equal, ALU.mult))
                link(dve.tensor_tensor(padrow[:, :], padrow[:, :], tab[:, 0, :], ALU.subtract))
                dve.tensor_scalar(rows[:, :], padrow[:, :], float(T), None, ALU.add).then_inc(rows_ready, 1)

            def factors():
                for m in range(2):
                    link(dve.tensor_tensor(bnm[:, :, :], bge[:, :, :], nexp[:, m, :].unsqueeze(1).to_broadcast([P, NB, E]), ALU.mult))
                    link(dve.tensor_reduce(bnx[:, m, :], bnm[:, :, :], AX.X, ALU.add))
                dve.tensor_scalar(silu_f[:, :].bitcast(i32), bnx[:, 0, :], 39.0, EXP, ALU.add, ALU.mult)
                dve.tensor_scalar(act_f[:, :].bitcast(i32), bnx[:, 0, :], -EXP, 181.0 * EXP, ALU.mult, ALU.add)
                link(dve.scalar_tensor_tensor(y_x[:, :], bnx[:, 0, :], 2.0, bnx[:, 1, :], ALU.mult, ALU.add))
                link(dve.tensor_scalar(y_x[:, :], y_x[:, :], -81.0, 0.0, ALU.add, ALU.max))
                link(dve.tensor_scalar(y_f[:, :].bitcast(i32), y_x[:, :], 254.0, EXP, ALU.min, ALU.mult))
                link(dve.tensor_tensor(y_f[:, :], y_f[:, :], tab[:, 1, :], ALU.mult))
                dve.tensor_scalar(y_fl[:, :], y_f[:, :], 1.0 / LOW, None, ALU.mult).then_inc(factors_ready, 1)

            def x_low(i, s):
                dve.wait_ge(xh_ready, i + 1)
                dve.scalar_tensor_tensor(xTl[s], bank[5][:, 0:D], H_SCALE, xTh[s], ALU.mult, ALU.subtract).then_inc(xl_ready, 1)

            routing = {4: [top_two], 7: [pick], 8: [scores], 9: [starts, slots], 10: [places, score_parts],
                       12: [loads, load_parts], 13: [block_experts], 15: [slot_rows], 22: [factors]}
            n_up = n_down = 0
            for s, (kind, hf, c) in enumerate(SLOTS):
                if kind == "up":
                    dve.wait_ge(ssilu_ready, n_up + 1)
                    dve.scalar_tensor_tensor(saT[:, c, :], bank[U_BANK[turn(hf, c)]][:, :], up_f[:, 1:2], sgs[turn(hf, c)],
                                             ALU.mult, ALU.mult).then_inc(sact_ready, 1)
                    n_up += 1
                if s == SECOND_HALF_SLOT:
                    hT_low(1)
                prepare(s, (2, scale1_of), (1, scale2_of), (0, low1_of), (0, high2_of))
                if s == 0:
                    norm_variance(HT, NT)
                    rsqrt(rh[:, HT:NT], var[:, HT:NT], HT, NT)
                    norm_offset(HT, NT)
                    normed(1)
                if kind == "down":
                    dve.wait_ge(sdown_done, n_down + 1)
                    dve.scalar_tensor_tensor(x_sb[:, n_down, :], bank[Y_BANK[n_down % 3]][:, 0:D], tanhs[:, 1:2], x_sb[:, n_down, :],
                                             ALU.mult, ALU.add).then_inc(sum_ready, 1)
                    n_down += 1
                if s - 1 in BLOCK_SLOTS:
                    i = BLOCK_SLOTS.index(s - 1)
                    x_low(i, i)
                for step in routing.get(s, ()):
                    step()

            def mult(i):
                dve.wait_ge(silu_ready, i + 1)
                dve.wait_ge(up_done, i + 1)
                dve.scalar_tensor_tensor(act[:, :], bank[2][:, :], act_f[:, bass.ds(i, 1)], sg, ALU.mult, ALU.mult).then_inc(act_ready, 1)

            def a_low(i):
                dve.wait_ge(ah_ready, i + 1)
                dve.scalar_tensor_tensor(aTl, aTh, -LOW, bank[6][:, :], ALU.mult, ALU.add).then_inc(al_ready, 1)

            def y_sum(i, s, added):
                dve.wait_ge(yhi_ready, i + 1)
                if added is not None:
                    dve.wait_ge(y_added, added)
                dve.scalar_tensor_tensor(ysb[s], bank[Y_BANK[s]][:, D:2 * D], y_fl[:, bass.ds(i, 1)], yhi[s],
                                         ALU.mult, ALU.add).then_inc(y_ready, 1)

            mult(0)
            for i in range(1, 4):
                x_low(i + 1, (i + 1) % 3)
                a_low(i - 1)
                mult(i)
                y_sum(i - 1, (i - 1) % 3, None)
            with dve.Fori(1, (NB - 2) // 3) as j:
                for u in range(3):
                    i = j * 3 + (u + 1)
                    x_low(i + 1, (u + 2) % 3)
                    a_low(i - 1)
                    mult(i)
                    y_sum(i - 1, u, (i - 3) * 16)
            i = NB - 1
            a_low(i - 1)
            mult(i)
            y_sum(i - 1, (i - 1) % 3, 16 * (i - 3))
            a_low(i)
            y_sum(i, i % 3, 16 * (i - 2))

        @block.scalar
        def _(se):
            def sq1_of(e):
                se.wait_ge(raw1_in[e % 2], 16 * KC * (e // 2 + 1))
                se.activation(w1h[:, e, :, :].rearrange("p k f -> p (k f)"), stage[:, e % 2, 0:N1], ACT.Square,
                              accum_out=sumsq[:, 0, e:e + 1]).then_inc(sq1_ready, 1)

            def sq2_of(e):
                se.wait_ge(raw2_in[e % 2], 16 * (e // 2 + 1))
                se.activation(w2h[:, e, :, :].rearrange("p c d -> p (c d)"), stage[:, e % 2, N1:], ACT.Square,
                              accum_out=sumsq[:, 1, e:e + 1]).then_inc(sq2_ready, 1)

            def high1_of(e):
                se.wait_ge(scale1_ready, e + 1)
                se.activation(w1h[:, e, :, :].rearrange("p k f -> p (k f)"), stage[:, e % 2, 0:N1], ACT.Copy,
                              scale=wscale[:, 0, e:e + 1]).then_inc(high1_ready, 1)

            def shared_square(m):
                se.wait_ge((wg_in, wu_in)[m], 16)
                se.activation(wsh[:, m, :, :].rearrange("p k f -> p (k f)"), raws[:, m * NS:(m + 1) * NS], ACT.Square,
                              accum_out=sumsq_s[:, m:m + 1]).then_inc(sqs_ready, 1)

            def shared_high(m):
                se.wait_ge(scaleds_ready, m + 1)
                se.activation(wsh[:, m, :, :].rearrange("p k f -> p (k f)"), raws[:, m * NS:(m + 1) * NS], ACT.Copy).then_inc(highs_ready, 1)

            se.wait_ge(kvc_done, 1)
            se.activation(kvc_sb[:, :, :].rearrange("p t c -> p (t c)"), bank[2][:, :], ACT.Copy).then_inc(kvc_ready, 1)
            for n in range(2):
                se.wait_ge(kvT_done, n + 1)
                se.activation(kvT_sb[:, n * 512:(n + 1) * 512], bank[n][0:C, :], ACT.Copy).then_inc(kvT_ready, 1)
            for n in range(2):
                se.wait_ge(oT_done, n + 1)
                se.activation(oT_sb[:, n * 512:(n + 1) * 512], bank[3 + n][0:C, :], ACT.Copy).then_inc(oT_ready, 1)
            se.wait_ge(gate_in, 80)
            se.activation(tanhs[:, :], gates[:, :], ACT.Tanh).then_inc(tanh_ready, 1)
            shared_square(0)
            shared_square(1)
            sq1_of(0)

            def scaled(a, b):
                se.wait_ge(rs_ready, a // HT + 1)
                for t in range(a, b):
                    se.wait_ge(zc_ready, t + 1)
                    se.activation(z_sb[:, t, :], z_sb[:, t, :], ACT.Copy, scale=rs[:, t:t + 1]).then_inc(zn_ready, 1)

            def exponentials(a, b):
                for t in range(a, b):
                    se.wait_ge(max_ready, t + 1)
                    se.activation(z_sb[:, t, :], z_sb[:, t, :], ACT.Exp, bias=nmax[:, t:t + 1], scale=-1.0,
                                  accum_out=esum[:, t:t + 1]).then_inc(exp_ready, 1)

            scaled(0, HT)
            exponentials(0, HT)
            shared_high(0)
            shared_high(1)
            scaled(HT, NT)

            def hT_high(hf):
                for k in range(KC):
                    se.wait_ge(hT_done, hf * KC + k + 1)
                    se.activation(hTh[:, k, hf * 512:(hf + 1) * 512], bank[(5, 4)[k]][:, :], ACT.Copy, scale=H_SCALE).then_inc(hTh_ready, 1)

            def hT_copy(hf):
                for k in range(KC):
                    se.wait_ge(hTl_ready, hf * KC + k + 1)
                    se.activation(hT32[hf][:, k, :], bank[(5, 4)[k]][:, :], ACT.Copy).then_inc(hT_ready, 1)

            def x_high(i, s):
                se.wait_ge(xT_done, i + 1)
                se.activation(xTh[s], bank[5][:, 0:D], ACT.Copy, scale=H_SCALE).then_inc(xh_ready, 1)

            hT_high(0)
            exponentials(HT, NT)
            hT_copy(0)
            n_up = 0
            for s, (kind, hf, c) in enumerate(SLOTS):
                if kind == "up":
                    se.wait_ge(sup_done, n_up + 1)
                    if c >= 2:
                        se.wait_ge(sact_ready, n_up - 2 if hf and c > 2 else n_up - 1)
                    se.activation(sgs[turn(hf, c)], bank[G_BANK[turn(hf, c)]][:, :], ACT.Silu, scale=up_f[:, 0:1]).then_inc(ssilu_ready, 1)
                    n_up += 1
                if s == SECOND_HALF_SLOT:
                    hT_high(1)
                    hT_copy(1)
                if s == SCORE_SLOT:
                    se.wait_ge(dlt_ready, 1)
                    se.activation(edlt[:, :], dlt[:, :], ACT.Exp).then_inc(edlt_ready, 1)
                if s - 1 in BLOCK_SLOTS:
                    i = BLOCK_SLOTS.index(s - 1)
                    x_high(i, i)
                prepare(s, (1, high1_of), (3, sq1_of), (2, sq2_of))

            def silu(i):
                se.wait_ge(gate_done, i + 1)
                se.activation(sg, bank[0][:, :], ACT.Silu, scale=silu_f[:, bass.ds(i, 1)]).then_inc(silu_ready, 1)

            def a_high(i):
                se.wait_ge(aT_done, i + 1)
                se.activation(aTh, bank[6][:, :], ACT.Copy, scale=1.0 / LOW).then_inc(ah_ready, 1)

            def y_high(i, s):
                se.wait_ge(y_done, i + 1)
                se.activation(yhi[s], bank[Y_BANK[s]][:, 0:D], ACT.Copy, scale=y_f[:, bass.ds(i, 1)]).then_inc(yhi_ready, 1)

            se.wait_ge(factors_ready, 1)
            silu(0)
            se.wait_ge(low1_ready, KC * E)
            se.wait_ge(low2_ready, E)
            with se.Fori(0, (NB - 2) // 3) as j:
                for u in range(3):
                    i = j * 3 + (u + 1)
                    x_high(i + 1, (u + 2) % 3)
                    a_high(i - 1)
                    silu(i)
                    y_high(i - 1, u)
            a_high(NB - 2)
            silu(NB - 1)
            y_high(NB - 2, (NB - 2) % 3)
            a_high(NB - 1)
            y_high(NB - 1, (NB - 1) % 3)

        @block.tensor
        def _(pe):
            def warm_up(n, b):
                for _ in range(n):
                    pe.matmul(bank[b][:, :], warm[:, 0:P], warm[:, :], start=True, stop=True)

            pe.wait_ge(warm_ready, 1)
            warm_up(13, 7)
            pe.wait_ge(wk_in, 32)
            pe.wait_ge(ctxc_ready, 1)
            for t in range(NT):
                last = pe.matmul(bank[2][:, t * C:(t + 1) * C], ctxc_sb[:, t * P:(t + 1) * P], wk_sb[0:C, :], start=True, stop=True)
            last.then_inc(kvc_done, 1)
            pe.wait_ge(ctx_in, 16)
            pe.wait_ge(ones_row, 1)
            for n in range(2):
                pe.matmul(bank[n][0:C, :], wk_sb[:, :], ctx_sb[:, n * 512:(n + 1) * 512], start=True, stop=True).then_inc(kvT_done, 1)
            pe.wait_ge(kvc_ready, 1)

            def ctx_rows(b):
                pe.wait_ge(xT_in[b // 2], 16)
                o = bank[3 + b // 2][0:C, (b % 2) * TB:(b % 2 + 1) * TB]
                for k in range(KC):
                    last = pe.matmul(o, kvc_sb[:, b * KC + k, :], xT_sb[:, k, b * TB:(b + 1) * TB], start=(k == 0), stop=(k == KC - 1))
                if b % 2:
                    last.then_inc(oT_done, 1)

            def similarity(t):
                pe.wait_ge(oT_ready, t // HT + 1)
                pe.wait_ge(kvT_ready, 2)
                b = t * P // TB
                last = pe.matmul(sim_of(t), oT_sb[:, t * P:(t + 1) * P], kvT_sb[:, b * TB:(b + 1) * TB], start=True, stop=True)
                if t % 2:
                    last.then_inc(sim_done, 1)

            for b in range(3):
                ctx_rows(b)
            for t in range(HT):
                similarity(t)
            ctx_rows(3)
            for t in range(HT, NT):
                similarity(t)
            pe.wait_ge(consts, 1)
            for m in range(2):
                pe.wait_ge(sqs_ready, m + 1)
                if m:
                    pe.wait_ge(scales_ready, m)
                pe.matmul(bank[6][:, 2 * E + m:2 * E + m + 1], ones[:, :], sumsq_s[:, m:m + 1], start=True, stop=True).then_inc(norms_done, 1)

            def norm1(e):
                pe.wait_ge(sq1_ready, e + 1)
                pe.wait_ge(scales_ready, 2)
                if e:
                    pe.wait_ge(scale2_ready, e)
                pe.matmul(bank[6][:, e:e + 1], ones[:, :], sumsq[:, 0, e:e + 1], start=True, stop=True).then_inc(norm1_done, 1)

            def norm2(e):
                pe.wait_ge(sq2_ready, e + 1)
                pe.wait_ge(scale1_ready, e + 1)
                pe.matmul(bank[6][:, E + e:E + e + 1], ones[:, :], sumsq[:, 1, e:e + 1], start=True, stop=True).then_inc(norm2_done, 1)

            def router(hf):
                pe.wait_ge(hT_ready, KC * (hf + 1))
                for t in range(HT):
                    tt = hf * HT + t
                    for k in range(KC):
                        last = pe.matmul(bank[3][:, tt * E:(tt + 1) * E], hT32[hf][:, k, t * P:(t + 1) * P], rw_sb[:, k, :],
                                         start=(k == 0), stop=(k == KC - 1))
                last.then_inc(logit_done, 1)

            def trans_h(hf):
                for t in range(HT):
                    if t == 0 and hf:
                        pe.wait_ge(hT_ready, KC)
                    pe.wait_ge(h_ready, hf * HT + t + 1)
                    for k in range(KC):
                        last = pe.transpose(bank[(5, 4)[k]][:, t * P:(t + 1) * P], h_sb[:, hf * HT + t, k * P:(k + 1) * P], ident[:, :])
                        if t == HT - 1:
                            last.then_inc(hT_done, 1)

            def prefix():
                pe.wait_ge(picks_ready, 1)
                NP = (NT + 1) * E
                pe.matmul(bank[5][:, 0:NP], before[:, :], picks[:, :, :].rearrange("p t e -> p (t e)"), start=True, stop=False)
                for t in range(NT):
                    last = pe.matmul(bank[5][:, (t + 1) * E:NP].rearrange("p (t e) -> p t e", e=E), ones_b[:, :],
                                     picks[:, t:t + 1, :].to_broadcast([P, NT - t, E]), start=False, stop=(t == NT - 1))
                last.then_inc(pre_done, 1)

            def table():
                pe.wait_ge(load_ready, 1)
                pe.wait_ge(parts_ready, 1)
                for n in range(TOPK * NT):
                    last = pe.matmul(bank[5][:, 0:4 * NB], hot_j[:, n, :], load[:, n, :, :].rearrange("p a b -> p (a b)"),
                                     start=(n == 0), stop=(n == TOPK * NT - 1))
                last.then_inc(tab_done, 1)

            def trans_x(i, s, count):
                pe.wait_ge(xg_in[s], count)
                if i is not None:
                    pe.wait_ge(xl_ready, i)
                for k in range(KC):
                    last = pe.transpose(bank[5][:, k * P:(k + 1) * P], xg[s][:, k * P:(k + 1) * P], ident[:, :])
                last.then_inc(xT_done, 1)

            pe.wait_ge(exp_ready, HT)
            warm_up(22, 2)
            trans_h(0)
            warm_up(10, 2)
            n_up = n_down = 0
            for s, (kind, hf, c) in enumerate(SLOTS):
                if kind == "up":
                    if c >= 2 + hf:
                        pe.wait_ge(sact_ready, n_up - 1 - hf)
                    if n_up == 0:
                        pe.wait_ge(lows_ready, 2)
                    if hf and c in (1, 2):
                        pe.wait_ge(sum_ready, 2 + c)
                    if n_up in (0, SC):
                        pe.wait_ge(hTl_ready, KC * (hf + 1))
                    cols = slice(hf * 512, (hf + 1) * 512)
                    for m, b in ((0, bank[G_BANK[turn(hf, c)]]), (1, bank[U_BANK[turn(hf, c)]])):
                        for k in range(KC):
                            wh_, wl_ = (w_[:, m, k, c * P:(c + 1) * P] for w_ in (wsh, wsl))
                            pe.matmul(b[:, :], wh_, hTh[:, k, cols], start=(k == 0), stop=False)
                            pe.matmul(b[:, :], wh_, hTl[:, k, cols], start=False, stop=False)
                            last = pe.matmul(b[:, :], wl_, hTh[:, k, cols], start=False, stop=(k == KC - 1))
                    last.then_inc(sup_done, 1)
                    n_up += 1
                else:
                    if c == 0:
                        pe.wait_ge(sact_ready, SC * (hf + 1) - 1)
                        pe.wait_ge(down_in, 16)
                    if n_down >= 3:
                        pe.wait_ge(sum_ready, n_down - 2)
                    for m in range(SC):
                        if c == 0 and m == SC - 1:
                            pe.wait_ge(sact_ready, SC * (hf + 1))
                        last = pe.matmul(bank[Y_BANK[n_down % 3]][:, 0:D], saT[:, m, c * P:(c + 1) * P], wd_sb[:, m, :],
                                         start=(m == 0), stop=(m == SC - 1))
                    last.then_inc(sdown_done, 1)
                    n_down += 1
                if s == ROUTER_SLOTS[0]:
                    router(0)
                if s == SECOND_HALF_SLOT:
                    trans_h(1)
                if s == ROUTER_SLOTS[1]:
                    router(1)
                if s == PREFIX_SLOT:
                    prefix()
                if s == TABLE_SLOT:
                    table()
                prepare(s, (2, norm1), (1, norm2))
                if s == BLOCK_SLOTS[0]:
                    pe.wait_ge(rows_ready, 1)
                    trans_x(None, 0, 16)
                if s == BLOCK_SLOTS[1]:
                    trans_x(1, 1, 16)

            pe.wait_ge(low1_ready, KC * E)
            pe.wait_ge(sact_ready, 2 * SC)

            def up_side(i, s, e, side):
                if side == 0:
                    pe.wait_ge(xl_ready, i + 1)
                for k in range(KC):
                    for x_, w_ in ((xTh, w1h), (xTh, w1l), (xTl, w1h)):
                        last = pe.matmul(bank[(0, 2)[side]][:, :], x_[s][:, k * P:(k + 1) * P],
                                         w_[:, bass.ds(e, 1), k, side * F:(side + 1) * F].rearrange("p a f -> p (a f)"),
                                         start=(k == 0 and x_ is xTh and w_ is w1h), stop=(k == KC - 1 and x_ is xTl))
                last.then_inc((gate_done, up_done)[side], 1)

            def up(i, s, e):
                up_side(i, s, e, 0)
                up_side(i, s, e, 1)

            def trans_a(i):
                pe.wait_ge(act_ready, i + 1)
                for c in range(FC):
                    last = pe.transpose(bank[6][:, c * P:(c + 1) * P], act[:, c * P:(c + 1) * P], ident[:, :])
                last.then_inc(aT_done, 1)

            def down(i, s, e, free):
                pe.wait_ge(al_ready, i + 1)
                if free is not None:
                    pe.wait_ge(y_ready, free)
                y = bank[Y_BANK[s]]
                for c in range(FC):
                    for w_ in (w2h, w2l):
                        pe.matmul(y[:, 0:D], aTh[:, c * P:(c + 1) * P], w_[:, bass.ds(e, 1), c, :].rearrange("p a d -> p (a d)"),
                                  start=(c == 0 and w_ is w2h), stop=(c == FC - 1 and w_ is w2l))
                for c in range(FC):
                    last = pe.matmul(y[:, D:2 * D], aTl[:, c * P:(c + 1) * P], w2h[:, bass.ds(e, 1), c, :].rearrange("p a d -> p (a d)"),
                                     start=(c == 0), stop=(c == FC - 1))
                last.then_inc(y_done, 1)

            def expert_of(i):
                return pe.value_load(bexpi[0:1, bass.ds(i, 1)], min_val=0, max_val=E - 1)

            up(0, 0, expert_of(0))
            pe.wait_ge(low2_ready, E)
            pe.wait_ge(sum_ready, NT)
            for i in range(1, 4):
                trans_x(i + 1, (i + 1) % 3, 16 * ((i + 1) // 3 + 1))
                trans_a(i - 1)
                up(i, i % 3, expert_of(i))
                down(i - 1, (i - 1) % 3, expert_of(i - 1), None)
            with pe.Fori(1, (NB - 2) // 3) as j:
                for u in range(3):
                    i = j * 3 + (u + 1)
                    if u == 0:
                        e_up = expert_of(i)
                    trans_x(i + 1, (u + 2) % 3, (j + (1 if u == 0 else 2)) * 16)
                    trans_a(i - 1)
                    up_side(i, (u + 1) % 3, e_up, 0)
                    if u == 0:
                        e_down = expert_of(i - 1)
                    if u < 2:
                        e_next = expert_of(i + 1)
                    up_side(i, (u + 1) % 3, e_up, 1)
                    down(i - 1, u, e_down, i - 3)
                    e_down, e_up = e_up, e_next
            i = NB - 1
            trans_a(i - 1)
            up(i, i % 3, expert_of(i))
            down(i - 1, (i - 1) % 3, expert_of(i - 1), i - 3)
            trans_a(i)
            down(i, i % 3, expert_of(i), i - 2)


_PAD = 128


def kernel(x, ctx_512, g_xattn, g_ffn, L0_xattn_W_k, L0_xattn_b_k, L0_xattn_ln_gamma, L0_xattn_ln_beta,
           L0_ffn_router_w, L0_ffn_w1, L0_ffn_w2, L0_ffn_w_gate, L0_ffn_w_up, L0_ffn_w_down):
    import numpy as np
    import concourse.bacc as bacc
    from concourse import mybir as mb
    from concourse.bass_utils import run_bass_kernel_spmd

    nc = bacc.Bacc("TRN2", target_bir_lowering=False, num_devices=1)
    B, S, D = x.shape
    x2 = np.ascontiguousarray(np.asarray(x).reshape(B * S, D))
    c2 = np.asarray(ctx_512).reshape(B * S, -1)
    ins = {
        "x": x2, "xT": x2.T, "ctxT": c2.T, "wkT": np.asarray(L0_xattn_W_k).T, "bk": L0_xattn_b_k,
        "gamma": L0_xattn_ln_gamma, "beta": L0_xattn_ln_beta, "g_att": g_xattn, "g_ffn": g_ffn,
        "rw": L0_ffn_router_w, "w1": L0_ffn_w1, "w2": L0_ffn_w2, "wg": L0_ffn_w_gate, "wu": L0_ffn_w_up, "wd": L0_ffn_w_down,
    }
    arrays, args = {}, []
    for name, a in ins.items():
        a = np.ascontiguousarray(a)
        arrays[f"in_{name}"] = a
        args.append(nc.dram_tensor(f"in_{name}", a.shape, mb.dt.from_np(a.dtype), kind="ExternalInput").ap())
    args.append(nc.dram_tensor("out_rows", (B * S + _PAD, D), mb.dt.float32, kind="ExternalOutput").ap())
    gated_attention_moe(nc, *args)
    r = run_bass_kernel_spmd(nc, [arrays], core_ids=[0])
    return r.results[0]["out_rows"][0:B * S].reshape(B, S, D)
```
